# Optimizing a Trainium2 kernel written in Bass

```python
import numpy as np
import jax
import jax.numpy as jnp

def _softmax(x, axis=-1):
    return jax.nn.softmax(x, axis=axis)
def _gelu(x):
    return jax.nn.gelu(x, approximate=True)
def _silu(x):
    return jax.nn.silu(x)
def _sigmoid(x):
    return jax.nn.sigmoid(x)
def _layernorm(x, axis=-1, eps=1e-5):
    m = jnp.mean(x, axis=axis, keepdims=True)
    v = jnp.var(x, axis=axis, keepdims=True)
    return (x - m) / jnp.sqrt(v + eps)
def _scatter_add(tgt, idx, src, axis=0):
    return tgt.at[idx].add(src)
def _segment_sum(src, seg, n):
    return jax.ops.segment_sum(src, seg, n)

kernel_name = 'mk_adj_preln_d2_adj_128_95fbd6'

def setup_inputs(seed: int = 0):
    np.random.seed(seed)
    _w = jnp.asarray
    def _rec_inputs():
        import jax
        import jax.numpy as jnp
        _gk = jax.random.key(seed)
        x = -0.000929 + 1 * jax.random.normal(jax.random.fold_in(_gk, 1), (8192, 128), jnp.float32)
        _a = jax.random.bernoulli(jax.random.fold_in(_gk, 2), 0.00195312, (8192, 8192))
        _a = jnp.logical_or(_a, jnp.swapaxes(_a, -1, -2))
        _a = jnp.logical_or(_a, jnp.eye(8192, dtype=bool))
        adj = _a.astype(jnp.int32)
        return x, adj
    x, adj = _rec_inputs()
    def _L0_gnn_setup():
        import jax
        import jax.numpy as jnp
        import numpy as np
        from jax import lax
        N = 8192
        F = 128
        CHUNK = 64
        key = jax.random.key(seed)
        kx, ka = jax.random.split(key)
        X = jax.random.normal(kx, (N, F), dtype=jnp.float32)
        adj = jax.random.randint(ka, (N, N), 0, 2, dtype=jnp.int32)
        return {'X': X, 'adj': adj}
    _L0_gnn_all = _L0_gnn_setup()
    _L0_gnn_in = {k: v for k, v in _L0_gnn_all.items() if k in ()}
    del _L0_gnn_all

    def _L1_gnn_setup():
        import jax, jax.numpy as jnp
        import numpy as np
        NEG_INF = -9000000000000000.0
        ALPHA = 0.2
        key = jax.random.key(seed)
        k1, k2, k3, k4 = jax.random.split(key, 4)
        N, F_IN, H, D = (8192, 128, 4, 32)
        h = jax.random.normal(k1, (N, F_IN), dtype=jnp.float32)
        adj = jax.random.randint(k2, (N, N), 0, 2, dtype=jnp.int32)
        W = jax.random.normal(k3, (F_IN, H * D), dtype=jnp.float32) * (1.0 / np.sqrt(F_IN))
        a = jax.random.normal(k4, (1, H, 2 * D), dtype=jnp.float32)
        return {'h': h, 'adj': adj, 'W': W, 'a': a}
    _L1_gnn_all = _L1_gnn_setup()
    _L1_gnn_in = {k: v for k, v in _L1_gnn_all.items() if k in ('W', 'a', )}
    del _L1_gnn_all

    return {
        "x": x,
        "adj": adj,
        "L1_gnn_W": _L1_gnn_in["W"],
        "L1_gnn_a": _L1_gnn_in["a"],
    }

def reference(x, adj, L1_gnn_W, L1_gnn_a):
    import jax
    import jax.numpy as jnp
    def _L0_gnn_ref(X, adj):
        import jax
        import jax.numpy as jnp
        import numpy as np
        from jax import lax
        N = 8192
        F = 128
        CHUNK = 64
        neg = jnp.finfo(X.dtype).min
        mask = adj != 0
        n, f = X.shape

        def body(_, mrows):
            vals = jnp.max(jnp.where(mrows[:, :, None], X[None, :, :], neg), axis=1)
            has_nbr = jnp.any(mrows, axis=1)
            return (None, jnp.where(has_nbr[:, None], vals, jnp.zeros((), X.dtype)))
        _, out = lax.scan(body, None, mask.reshape(n // CHUNK, CHUNK, n))
        return out.reshape(n, f)

    def _L1_gnn_ref(h, adj, W, a):
        import jax, jax.numpy as jnp
        import numpy as np
        NEG_INF = -9000000000000000.0
        ALPHA = 0.2
        N = h.shape[0]
        H = a.shape[1]
        D = a.shape[2] // 2
        Wh = (h @ W).reshape(N, H, D)
        a_src = a[0, :, :D]
        a_dst = a[0, :, D:]
        s_src = jnp.einsum('nhd,hd->nh', Wh, a_src)
        s_dst = jnp.einsum('nhd,hd->nh', Wh, a_dst)
        e = s_src[:, None, :] + s_dst[None, :, :]
        e = jnp.where(e >= 0, e, ALPHA * e)
        e = jnp.where(adj[:, :, None] > 0, e, NEG_INF)
        attention = jax.nn.softmax(e, axis=1)
        h_prime = jnp.einsum('ijh,jhd->ihd', attention, Wh)
        return jax.nn.elu(h_prime.reshape(N, H * D))

    h = jnp.maximum(_layernorm(x, axis=-1), 0.0)
    x = x + _L0_gnn_ref(h, adj)
    h = jnp.maximum(_layernorm(x, axis=-1), 0.0)
    x = x + _L1_gnn_ref(h, adj, L1_gnn_W, L1_gnn_a)
    return x


_drawn_inputs = setup_inputs


def setup_inputs(seed=0):
    import zlib

    import numpy as np

    out = dict(_drawn_inputs(seed))
    spreads = {}
    factors = {}
    for name, (base, spread) in spreads.items():
        noise = np.random.default_rng([zlib.crc32(name.encode()), seed]).standard_normal(out[name].shape)
        drawn = base * np.exp(spread * noise) if base else spread * noise
        out[name] = jnp.asarray(drawn.astype(out[name].dtype))
    for name, factor in factors.items():
        out[name] = (out[name] * factor).astype(out[name].dtype)
    return out
```

```python
from contextlib import ExitStack

import concourse.bass as bass
import concourse.mybir as mybir

NODES = 8192
FEAT = 128
HEADS = 4
HDIM = FEAT // HEADS
ROWS = 128
TILES = NODES // ROWS
CHUNK = 128
CHUNKS = NODES // CHUNK
SLOTS = 64
ROUNDS = SLOTS // 8
GROW = FEAT + HEADS
BLOCK = SLOTS
BLOCKS = NODES // BLOCK
EPS = 1e-5
SLOPE = 0.2
MASKED = 9.0e15
PAD_SCORE = -1.0e17
ALL = 16


def gnn_program(nc, x, adj, weight, attn, out):
    f32, bf16, i32, u32 = mybir.dt.float32, mybir.dt.bfloat16, mybir.dt.int32, mybir.dt.uint32
    ALU, ACT, AX = mybir.AluOpType, mybir.ActivationFunctionType, mybir.AxisListType

    node_table = nc.dram_tensor("node_table", (NODES + 1, FEAT), f32).ap()
    attn_table = nc.dram_tensor("attn_table", (NODES + 1, GROW), f32).ap()
    mid = nc.dram_tensor("mid", (NODES, FEAT), f32).ap()

    ctx = ExitStack()
    with ctx:
        def sb(name, shape, dt=f32):
            return ctx.enter_context(nc.sbuf_tensor(name, shape, dt))

        def ps(name, shape):
            return ctx.enter_context(nc.psum_tensor(name, shape, f32))

        def sem(name):
            return ctx.enter_context(nc.semaphore(name))

        adj_in = [sb(f"adj_in{b}", [ROWS, NODES], i32) for b in range(2)]
        keys = sb("keys", [ROWS, NODES], bf16)
        squares = sb("squares", [ROWS, NODES], bf16)
        gath = [sb(f"gath{b}", [ROWS, SLOTS, GROW]) for b in range(2)]
        lists = sb("lists", [ROWS, TILES, SLOTS], u32)
        stage = [sb(f"stage{b}", [ROWS, SLOTS], u32) for b in range(2)]
        column_number = sb("column_number", [ROWS, CHUNK], bf16)
        chunk_base = sb("chunk_base", [ROWS, CHUNKS])
        cand = sb("cand", [ROWS, CHUNKS, 8])
        cand_base = sb("cand_base", [ROWS, CHUNKS, 8])
        top = sb("top", [ROWS, SLOTS])
        is_nb = sb("is_nb", [ROWS, SLOTS])
        square_sum = sb("square_sum", [ROWS, TILES])
        listed = sb("listed", [ROWS, TILES])
        x_t = [sb(f"x_t{b}", [ROWS, FEAT]) for b in range(2)]
        mid_t = [sb(f"mid_t{b}", [ROWS, FEAT]) for b in range(2)]
        row_t = [sb(f"row_t{b}", [ROWS, GROW]) for b in range(2)]
        src_score = sb("src_score", [ROWS, TILES, HEADS])
        nb_max = sb("nb_max", [ROWS, FEAT])
        bn = sb("bn", [ROWS, 6])
        mean_var = sb("mean_var", [ROWS, 2])
        std = sb("std", [ROWS, 1])
        rstd = sb("rstd", [ROWS, 1])
        shift = sb("shift", [ROWS, 1])
        normed = sb("normed", [ROWS, FEAT])
        normed_T = sb("normed_T", [FEAT, ROWS])
        stat = sb("stat", [ROWS, TILES])
        stat_r = sb("stat_r", [ROWS, TILES])
        eps_t = sb("eps_t", [ROWS, 1])
        quarter = sb("quarter", [ROWS, 1])
        ones = sb("ones", [ROWS, 1])
        ident = sb("ident", [ROWS, ROWS])
        w_cat = sb("w_cat", [FEAT, FEAT + 2 * HEADS])
        w_T = sb("w_T", [FEAT, FEAT])
        a_blocks = sb("a_blocks", [FEAT, 2 * HEADS])
        pad_row = sb("pad_row", [1, GROW])
        score = sb("score", [ROWS, HEADS, SLOTS])
        prob = sb("prob", [ROWS, HEADS, SLOTS])
        peak = sb("peak", [ROWS, HEADS])
        total = sb("total", [ROWS, HEADS])
        agg = sb("agg", [ROWS, FEAT])
        neg = sb("neg", [ROWS, FEAT])
        neg_exp = sb("neg_exp", [ROWS, FEAT])
        pos = sb("pos", [ROWS, FEAT])
        out_t = [sb(f"out_t{b}", [ROWS, FEAT]) for b in range(2)]
        bad = sb("bad", [ROWS, TILES])
        bad_row = sb("bad_row", [ROWS, 1])
        bad_count = sb("bad_count", [1, 1], i32)
        peak_new = sb("peak_new", [ROWS, HEADS])
        rescale = sb("rescale", [ROWS, HEADS])
        part = sb("part", [ROWS, FEAT])
        part_sum = sb("part_sum", [ROWS, HEADS])

        p_T = ps("p_T", [FEAT, ROWS])
        p_row = ps("p_row", [ROWS, FEAT + 2 * HEADS])
        p_w = ps("p_w", [FEAT, FEAT])
        p_a = ps("p_a", [FEAT, 2 * HEADS])
        p_bad = ps("p_bad", [1, 1])

        weights_loaded = sem("weights_loaded")
        a_zeroed = sem("a_zeroed")
        a_loaded = sem("a_loaded")
        all_x_loaded = sem("all_x_loaded")
        const_made = sem("const_made")
        pad_made = sem("pad_made")
        pads_stored = sem("pads_stored")
        setup = sem("setup")
        var_made = sem("var_made")
        std_made = sem("std_made")
        nodes_normed = sem("nodes_normed")
        nodes_relued = sem("nodes_relued")
        nodes_stored = sem("nodes_stored")
        wT_done = sem("wT_done")
        wT_copied = sem("wT_copied")
        wa_done = sem("wa_done")
        w_ready = sem("w_ready")
        adj_loaded = [sem(f"adj_loaded{b}") for b in range(2)]
        x_loaded = [sem(f"x_loaded{b}") for b in range(2)]
        cast_done = sem("cast_done")
        squares_done = sem("squares_done")
        keys_used = sem("keys_used")
        build_step = sem("build_step")
        list_ready = sem("list_ready")
        gathered = [sem(f"gathered{b}") for b in range(2)]
        gath_free = sem("gath_free")
        pool_turns = sem("pool_turns")
        post_step = sem("post_step")
        tile_var = sem("tile_var")
        tile_std = sem("tile_std")
        shift_made = sem("shift_made")
        mid_made = sem("mid_made")
        tile_normed = sem("tile_normed")
        transposed = sem("transposed")
        T_copied = sem("T_copied")
        projected = sem("projected")
        row_made = sem("row_made")
        row_stored = [sem(f"row_stored{b}") for b in range(2)]
        mid_stored = [sem(f"mid_stored{b}") for b in range(2)]
        check_step = sem("check_step")
        bad_row_made = sem("bad_row_made")
        bad_summed = sem("bad_summed")
        verdict = sem("verdict")
        stage_ready = sem("stage_ready")
        attn_gathered = [sem(f"attn_gathered{b}") for b in range(2)]
        attn_gath_free = sem("attn_gath_free")
        attn_step = sem("attn_step")
        score_made = sem("score_made")
        prob_made = sem("prob_made")
        neg_made = sem("neg_made")
        neg_exped = sem("neg_exped")
        mid_loaded = [sem(f"mid_loaded{b}") for b in range(2)]
        out_made = sem("out_made")
        out_stored = [sem(f"out_stored{b}") for b in range(2)]
        dense_adj_loaded = sem("dense_adj_loaded")
        dense_mask_free = sem("dense_mask_free")
        dense_loaded = [sem(f"dense_loaded{b}") for b in range(2)]
        dense_free = sem("dense_free")
        dense_step = sem("dense_step")
        dense_score = sem("dense_score")
        dense_exp = sem("dense_exp")

        block = ctx.enter_context(nc.Block())

        adj_rows = adj.rearrange("(t p) n -> t p n", p=ROWS)
        x_rows = x.rearrange("(t p) f -> t p f", p=ROWS)
        mid_rows = mid.rearrange("(t p) f -> t p f", p=ROWS)
        out_rows = out.rearrange("(t p) f -> t p f", p=ROWS)
        node_rows = node_table[1:NODES + 1, :].rearrange("(t p) f -> t p f", p=ROWS)
        attn_rows = attn_table[1:NODES + 1, :].rearrange("(t p) f -> t p f", p=ROWS)
        node_blocks = node_table[1:NODES + 1, :].rearrange("(c k) f -> c k f", k=BLOCK)
        attn_blocks = attn_table[1:NODES + 1, :].rearrange("(c k) f -> c k f", k=BLOCK)
        all_x = gath[0][:, 0:TILES, 0:FEAT]
        all_sq = gath[1][:, 0:TILES, 0:FEAT]

        def tile_of(rows, t):
            return rows[bass.ds(t, 1), :, :].rearrange("o p f -> (o p) f")

        def stepper(engine, semaphore):
            count = [0]
            engine.sem_clear(semaphore)

            def step(ins):
                count[0] += 1
                ins.then_inc(semaphore, 1)
                engine.wait_ge(semaphore, count[0])
            return step, count

        def pairs(engine, body, first, last):
            with engine.Fori(first // 2, last // 2) as u:
                for b in range(2):
                    body(2 * u + b, u, b)

        @block.sync
        def _(sp):
            sp.dma_start(all_x, x.rearrange("(t p) f -> p t f", p=ROWS)).then_inc(all_x_loaded, ALL)
            sp.dma_start(w_cat[:, 0:FEAT], weight).then_inc(weights_loaded, ALL)
            sp.wait_ge(a_zeroed, 1)
            for h in range(HEADS):
                for col, lo in ((h, HDIM), (HEADS + h, 0)):
                    sp.dma_start(a_blocks[h * HDIM:(h + 1) * HDIM, col:col + 1],
                                 attn[0, h, lo:lo + HDIM].unsqueeze(1)).then_inc(a_loaded, ALL)

            def load(t, u, b, first=False):
                if not first:
                    sp.wait_ge(squares_done, t - 1)
                    sp.wait_ge(cast_done, t - 1)
                sp.dma_start(adj_in[b][:], tile_of(adj_rows, t)).then_inc(adj_loaded[b], ALL)

            def load_x(t, s, b, first=False):
                if not first:
                    sp.wait_ge(mid_made, s - 1)
                sp.dma_start(x_t[b][:], tile_of(x_rows, t)).then_inc(x_loaded[b], ALL)

            def store(t, s, b):
                sp.wait_ge(mid_made, s + 1)
                sp.dma_start(tile_of(mid_rows, t), mid_t[b][:]).then_inc(mid_stored[b], ALL)
                sp.wait_ge(row_made, s + 1)
                sp.dma_start(tile_of(attn_rows, t), row_t[b][:]).then_inc(row_stored[b], ALL)

            for b in range(2):
                load(b, 0, b, first=True)
                load_x(b, b, b, first=True)
            sp.wait_ge(pad_made, 2)
            sp.dma_start(node_table[0:1, :], pad_row[:, 0:FEAT]).then_inc(pads_stored, ALL)
            sp.dma_start(attn_table[0:1, :], pad_row[:, :]).then_inc(pads_stored, ALL)
            sp.wait_ge(nodes_relued, 1)
            sp.dma_start(node_table[1:NODES + 1, :].rearrange("(t p) f -> p t f", p=ROWS), all_x).then_inc(nodes_stored, ALL)

            def turn(t, u, b):
                load(t + 2, u + 1, b)
                store(t, t, b)
                load_x(t + 2, t + 2, b)
            pairs(sp, turn, 0, TILES - 2)
            for b in range(2):
                store(TILES - 2 + b, TILES - 2 + b, b)

            def load_mid(t, u, b, first=False):
                if not first:
                    sp.wait_ge(out_made, t - 1)
                sp.dma_start(mid_t[b][:], tile_of(mid_rows, t)).then_inc(mid_loaded[b], ALL)

            def store_out(t, u, b):
                sp.wait_ge(out_made, t + 1)
                sp.dma_start(tile_of(out_rows, t), out_t[b][:]).then_inc(out_stored[b], ALL)

            def attention_io():
                for b in range(2):
                    load_mid(b, 0, b, first=True)

                def attn_turn(t, u, b):
                    store_out(t, u, b)
                    load_mid(t + 2, u + 1, b)
                pairs(sp, attn_turn, 0, TILES - 2)
                for b in range(2):
                    store_out(TILES - 2 + b, TILES // 2 - 1, b)

            for b in range(2):
                sp.wait_ge(mid_stored[b], ALL * TILES // 2)
                sp.wait_ge(row_stored[b], ALL * TILES // 2)
            sp.wait_ge(verdict, 1)
            bad_rows = sp.value_load(bad_count[0:1, 0:1], min_val=0, max_val=ROWS)
            with sp.If(bad_rows == 0):
                attention_io()
            with sp.Else():
                def dense_blocks(t_all, rows_of, width):
                    with sp.Fori(0, BLOCKS // 2) as c2:
                        for b in range(2):
                            n = t_all * BLOCKS + 2 * c2 + b
                            sp.wait_ge(dense_free, n + 1)
                            src = rows_of[bass.ds(2 * c2 + b, 1), :, :].rearrange("o k f -> (o k) f")
                            sp.dma_start(gath[b][:, :, 0:width], src.unsqueeze(0).to_broadcast([ROWS, BLOCK, width])).then_inc(dense_loaded[b], ALL)

                with sp.Fori(0, TILES) as t:
                    sp.wait_ge(dense_mask_free, t + 1)
                    sp.dma_start(adj_in[0][:], tile_of(adj_rows, t)).then_inc(dense_adj_loaded, ALL)
                    sp.dma_start(x_t[0][:], tile_of(x_rows, t)).then_inc(x_loaded[0], ALL)
                    dense_blocks(t, node_blocks, FEAT)
                    s = t + TILES
                    sp.wait_ge(mid_made, s + 1)
                    sp.dma_start(tile_of(mid_rows, t), mid_t[0][:]).then_inc(mid_stored[0], ALL)
                    sp.wait_ge(row_made, s + 1)
                    sp.dma_start(tile_of(attn_rows, t), row_t[0][:]).then_inc(row_stored[0], ALL)
                sp.wait_ge(mid_stored[0], ALL * (TILES // 2 + TILES))
                sp.wait_ge(row_stored[0], ALL * (TILES // 2 + TILES))
                with sp.Fori(0, TILES) as t:
                    sp.wait_ge(dense_mask_free, t + TILES + 1)
                    sp.dma_start(adj_in[0][:], tile_of(adj_rows, t)).then_inc(dense_adj_loaded, ALL)
                    sp.dma_start(mid_t[0][:], tile_of(mid_rows, t)).then_inc(mid_loaded[0], ALL)
                    dense_blocks(t + TILES, attn_blocks, GROW)
                    sp.wait_ge(out_made, t + 1)
                    sp.dma_start(tile_of(out_rows, t), out_t[0][:]).then_inc(out_stored[0], ALL)
                sp.wait_ge(out_stored[0], ALL * TILES)
                sp.sem_inc(out_stored[1], ALL * (TILES // 2))
            for b in range(2):
                sp.wait_ge(out_stored[b], ALL * TILES // 2)

        @block.gpsimd
        def _(pool):
            pool.memset(a_blocks[:], 0.0).then_inc(a_zeroed, 1)
            pool.iota(column_number[:], pattern=[[1, CHUNK]], base=1, channel_multiplier=0,
                      allow_small_or_imprecise_dtypes=True).then_inc(const_made, 1)
            pool.iota(chunk_base[:], pattern=[[CHUNK, CHUNKS]], base=0, channel_multiplier=0,
                      allow_small_or_imprecise_dtypes=True).then_inc(const_made, 1)
            pool.memset(ident[:], 0.0).then_inc(const_made, 1)
            pool.wait_ge(const_made, 3)
            pool.affine_select(out=ident[:], in_=ident[:], compare_op=ALU.not_equal, fill=1.0, base=0,
                               pattern=[[-1, ROWS]], channel_multiplier=1).then_inc(const_made, 1)
            pool.memset(eps_t[:], EPS).then_inc(const_made, 1)
            pool.memset(quarter[:], -0.25).then_inc(const_made, 1)
            pool.memset(ones[:], 1.0).then_inc(const_made, 1)
            pool.memset(pad_row[:, 0:FEAT], 0.0).then_inc(pad_made, 1)
            pool.memset(pad_row[:, FEAT:GROW], PAD_SCORE).then_inc(pad_made, 1)
            pool.wait_ge(nodes_stored, ALL)
            pool.wait_ge(pads_stored, 2 * ALL)

            def gather(table, width, b, done):
                for k in range(SLOTS):
                    pool.indirect_dma_start(gath[b][:, k, 0:width], None, table,
                                            bass.IndirectOffsetOnAxis(ap=stage[b][:, k:k + 1], axis=0)).then_inc(done, ALL)

            def max_turn(t, u, b, first=False):
                if not first:
                    pool.wait_ge(gath_free, t - 1)
                    pool.sem_inc(pool_turns, 1)
                pool.wait_ge(list_ready, t + 1)
                pool.sem_inc(pool_turns, 1)
                gather(node_table, FEAT, b, gathered[b])
            for b in range(2):
                max_turn(b, 0, b, first=True)
            pairs(pool, max_turn, 2, TILES)

            pool.wait_ge(verdict, 1)
            bad_rows = pool.value_load(bad_count[0:1, 0:1], min_val=0, max_val=ROWS)
            with pool.If(bad_rows == 0):
                for b in range(2):
                    pool.wait_ge(mid_stored[b], ALL * TILES // 2)
                    pool.wait_ge(row_stored[b], ALL * TILES // 2)

                def attn_turn(t, u, b, first=False):
                    if not first:
                        pool.wait_ge(attn_gath_free, t - 1)
                        pool.sem_inc(pool_turns, 1)
                    pool.wait_ge(stage_ready, t + 1)
                    pool.sem_inc(pool_turns, 1)
                    gather(attn_table, GROW, b, attn_gathered[b])
                for b in range(2):
                    attn_turn(b, 0, b, first=True)
                pairs(pool, attn_turn, 2, TILES)
            with pool.Else():
                pool.nop()

        @block.tensor
        def _(pe):
            pe.wait_ge(const_made, 7)
            pe.wait_ge(weights_loaded, ALL)
            nc.tensor.transpose(p_w[:], w_cat[:, 0:FEAT], ident[:]).then_inc(wT_done, 1)
            pe.wait_ge(wT_copied, 1)
            pe.wait_ge(a_loaded, ALL * 2 * HEADS)
            nc.tensor.matmul(p_a[:], w_T[:], a_blocks[:], start=True, stop=True).then_inc(wa_done, 1)
            pe.wait_ge(w_ready, 1)

            def project(s):
                pe.wait_ge(tile_normed, s + 1)
                nc.tensor.transpose(p_T[:], normed[:], ident[:]).then_inc(transposed, 1)
                pe.wait_ge(T_copied, s + 1)
                nc.tensor.matmul(p_row[:], normed_T[:], w_cat[:], start=True, stop=True).then_inc(projected, 1)
            with pe.Fori(0, TILES) as t:
                project(t)
            pe.wait_ge(bad_row_made, 1)
            nc.tensor.matmul(p_bad[:], bad_row[:], ones[:], start=True, stop=True).then_inc(bad_summed, 1)
            pe.wait_ge(verdict, 1)
            bad_rows = pe.value_load(bad_count[0:1, 0:1], min_val=0, max_val=ROWS)
            with pe.If(bad_rows == 0):
                pe.nop()
            with pe.Else():
                with pe.Fori(0, TILES) as t:
                    project(t + TILES)

        @block.scalar
        def _(act):
            act.wait_ge(const_made, 7)
            act.wait_ge(wT_done, 1)
            nc.scalar.activation(w_T[:], p_w[:], ACT.Copy).then_inc(wT_copied, 1)
            act.wait_ge(wa_done, 1)
            act.wait_ge(weights_loaded, ALL)
            nc.scalar.activation(w_cat[:, FEAT:], p_a[:], ACT.Copy).then_inc(w_ready, 1)
            act.wait_ge(var_made, 1)
            nc.scalar.activation(stat_r[:], stat[:], ACT.Sqrt, bias=eps_t[:], scale=1.0 / FEAT).then_inc(std_made, 1)
            act.wait_ge(nodes_normed, 1)
            nc.scalar.activation(all_x, all_x, ACT.Relu).then_inc(nodes_relued, 1)

            def read_adj(t, u, b, first=False):
                act.wait_ge(adj_loaded[b], ALL * (u + 1))
                if not first:
                    act.wait_ge(keys_used, t)
                    act.wait_ge(squares_done, t)
                nc.scalar.activation(keys[:], adj_in[b][:], ACT.Copy).then_inc(cast_done, 1)
                nc.scalar.activation(squares[:], adj_in[b][:], ACT.Square, bias=quarter[:],
                                     accum_out=square_sum[:, bass.ds(t, 1)]).then_inc(squares_done, 1)

            def norm_and_row(t, s, b, prior):
                act.wait_ge(tile_var, s + 1)
                nc.scalar.activation(std[:], mean_var[:, 1:2], ACT.Sqrt, bias=eps_t[:]).then_inc(tile_std, 1)
                act.wait_ge(shift_made, s + 1)
                nc.scalar.activation(normed[:], mid_t[b][:], ACT.Relu, bias=shift[:], scale=rstd[:]).then_inc(tile_normed, 1)
                act.wait_ge(transposed, s + 1)
                nc.scalar.activation(normed_T[:], p_T[:], ACT.Copy).then_inc(T_copied, 1)
                act.wait_ge(projected, s + 1)
                if prior is not None:
                    act.wait_ge(row_stored[b], prior)
                nc.scalar.activation(row_t[b][:], p_row[:, 0:GROW], ACT.Copy)
                nc.scalar.activation(src_score[:, bass.ds(t, 1), :].rearrange("p o h -> p (o h)"),
                                     p_row[:, GROW:], ACT.Copy).then_inc(row_made, 1)

            read_adj(0, 0, 0, first=True)
            read_adj(1, 0, 1)
            norm_and_row(0, 0, 0, None)
            read_adj(2, 1, 0)
            norm_and_row(1, 1, 1, None)

            def turn(t, u, b):
                read_adj(t + 1, (u if b == 0 else u + 1), 1 - b)
                norm_and_row(t, t, b, ALL * u)
            pairs(act, turn, 2, TILES - 2)
            read_adj(TILES - 1, TILES // 2 - 1, 1)
            for b in range(2):
                norm_and_row(TILES - 2 + b, TILES - 2 + b, b, ALL * (TILES // 2 - 1))

            act.wait_ge(verdict, 1)
            bad_rows = act.value_load(bad_count[0:1, 0:1], min_val=0, max_val=ROWS)

            def elu_exp(t):
                act.wait_ge(neg_made, t + 1)
                nc.scalar.activation(neg_exp[:], neg[:], ACT.Exp).then_inc(neg_exped, 1)

            with act.If(bad_rows == 0):
                with act.Fori(0, TILES) as t:
                    act.wait_ge(score_made, t + 1)
                    nc.scalar.activation(prob[:], score[:], ACT.Exp).then_inc(prob_made, 1)
                    elu_exp(t)
            with act.Else():
                with act.Fori(0, TILES) as t:
                    norm_and_row(t, t + TILES, 0, ALL * TILES // 2 + ALL * t)
                with act.Fori(0, TILES) as t:
                    with act.Fori(0, BLOCKS) as c:
                        n = t * BLOCKS + c
                        act.wait_ge(dense_score, n + 1)
                        nc.scalar.activation(prob[:], score[:], ACT.Exp)
                        nc.scalar.activation(rescale[:], peak[:], ACT.Exp).then_inc(dense_exp, 1)
                    elu_exp(t)

        @block.vector
        def _(dve):
            V = nc.vector
            step, _ = stepper(dve, setup)
            dve.wait_ge(all_x_loaded, ALL)
            step(V.tensor_reduce(stat[:], all_x, AX.X, ALU.add))
            step(V.tensor_scalar(stat[:], stat[:], 1.0 / FEAT, None, ALU.mult))
            mean_b = stat[:].unsqueeze(2).to_broadcast([ROWS, TILES, FEAT])
            step(V.tensor_tensor(all_x, all_x, mean_b, ALU.subtract))
            step(V.tensor_tensor(all_sq, all_x, all_x, ALU.mult))
            V.tensor_reduce(stat[:], all_sq, AX.X, ALU.add).then_inc(var_made, 1)
            dve.wait_ge(std_made, 1)
            step(V.reciprocal(stat_r[:], stat_r[:]))
            rstd_b = stat_r[:].unsqueeze(2).to_broadcast([ROWS, TILES, FEAT])
            V.tensor_tensor(all_x, all_x, rstd_b, ALU.mult).then_inc(nodes_normed, 1)
            dve.wait_ge(const_made, 7)

            def build(t, b, first=False):
                step, count = stepper(dve, build_step)
                dve.wait_ge(cast_done, t + 1)
                by_chunk = keys[:].rearrange("p (c n) -> p c n", n=CHUNK)
                step(V.tensor_tensor(by_chunk, by_chunk,
                                     column_number[:].unsqueeze(1).to_broadcast([ROWS, CHUNKS, CHUNK]), ALU.mult))
                for c in range(CHUNKS):
                    last = V.max(cand[:, c, :], by_chunk[:, c, :])
                last.then_inc(keys_used, 1)
                dve.wait_ge(keys_used, t + 1)
                base_b = chunk_base[:].unsqueeze(2).to_broadcast([ROWS, CHUNKS, 8])
                step(V.scalar_tensor_tensor(cand_base[:], cand[:], 0.0, base_b, ALU.is_gt, ALU.mult))
                step(V.tensor_tensor(cand[:], cand[:], cand_base[:], ALU.add))
                flat = cand[:].rearrange("p c k -> p (c k)")
                for r in range(ROUNDS):
                    eight = top[:, 8 * r:8 * r + 8]
                    step(V.max(eight, flat))
                    if r < ROUNDS - 1:
                        step(V.match_replace(flat, eight, flat, 0.0))
                if not first:
                    dve.wait_ge(gathered[b], (t // 2) * SLOTS * ALL if isinstance(t, int) else ((t - b) // 2) * SLOTS * ALL)
                step(V.tensor_copy(stage[b][:], top[:]))
                V.tensor_scalar(is_nb[:], top[:], 0.0, 0.0, ALU.is_gt, ALU.add, accum_out=listed[:, bass.ds(t, 1)])
                step(V.tensor_copy(lists[:, bass.ds(t, 1), :].rearrange("p o k -> p (o k)"), stage[b][:]))
                dve.sem_inc(list_ready, 1)

            def post(s, b, prior_mid, step):
                if prior_mid is not None:
                    dve.wait_ge(mid_stored[b], prior_mid)
                V.tensor_tensor(mid_t[b][:], x_t[b][:], nb_max[:], ALU.add).then_inc(mid_made, 1)
                dve.wait_ge(mid_made, s + 1)
                step(V.bn_stats(bn[:], mid_t[b][:]))
                V.bn_aggr(mean_var[:], bn[:]).then_inc(tile_var, 1)
                dve.wait_ge(tile_std, s + 1)
                step(V.reciprocal(rstd[:], std[:]))
                V.scalar_tensor_tensor(shift[:], mean_var[:, 0:1], -1.0, rstd[:], ALU.mult, ALU.mult).then_inc(shift_made, 1)

            def reduce_max(t, u, b):
                step, _ = stepper(dve, post_step)
                dve.wait_ge(gathered[b], ALL * SLOTS * (u + 1))
                V.tensor_reduce(nb_max[:], gath[b][:, :, 0:FEAT].rearrange("p k f -> p f k"), AX.X, ALU.max).then_inc(gath_free, 1)
                dve.wait_ge(gath_free, t + 1)
                dve.wait_ge(x_loaded[b], ALL * (u + 1))
                return step

            build(0, 0, first=True)
            build(1, 1, first=True)
            post(0, 0, None, reduce_max(0, 0, 0))
            build(2, 0)
            post(1, 1, None, reduce_max(1, 0, 1))

            def turn(t, u, b):
                build(t + 1, 1 - b)
                post(t, b, ALL * u, reduce_max(t, u, b))
            pairs(dve, turn, 2, TILES - 2)
            build(TILES - 1, 1)
            for b in range(2):
                step = reduce_max(TILES - 2 + b, TILES // 2 - 1, b)
                post(TILES - 2 + b, b, ALL * (TILES // 2 - 1), step)

            step, count = stepper(dve, check_step)
            dve.wait_ge(squares_done, TILES)
            step(V.tensor_scalar(bad[:], listed[:], 0.5, NODES / 16, ALU.mult, ALU.add))
            step(V.tensor_tensor(bad[:], bad[:], square_sum[:], ALU.not_equal))
            step(V.tensor_scalar(is_nb[:], listed[:], 0.0, None, ALU.is_equal))
            step(V.tensor_tensor(bad[:], bad[:], is_nb[:], ALU.max))
            step(V.tensor_reduce(bad_row[:], bad[:], AX.X, ALU.max))
            dve.sem_inc(bad_row_made, 1)
            dve.wait_ge(bad_summed, 1)
            V.tensor_copy(bad_count[:], p_bad[:]).then_inc(verdict, 1)
            dve.wait_ge(verdict, 1)
            bad_rows = dve.value_load(bad_count[0:1, 0:1], min_val=0, max_val=ROWS)

            def heads(v):
                return v[:].unsqueeze(2).to_broadcast([ROWS, HEADS, SLOTS])

            def finish(t, b, step, prior):
                step(V.reciprocal(total[:], total[:]))
                agg_h = agg[:].rearrange("p (h d) -> p h d", h=HEADS)
                step(V.tensor_tensor(agg_h, agg_h, total[:].unsqueeze(2).to_broadcast([ROWS, HEADS, HDIM]), ALU.mult))
                V.tensor_scalar(neg[:], agg[:], 0.0, None, ALU.min).then_inc(neg_made, 1)
                step(V.scalar_tensor_tensor(pos[:], agg[:], 0.0, mid_t[b][:], ALU.max, ALU.add))
                dve.wait_ge(neg_exped, t + 1)
                if prior is not None:
                    dve.wait_ge(out_stored[b], prior)
                V.scalar_tensor_tensor(out_t[b][:], neg_exp[:], -1.0, pos[:], ALU.add, ALU.add).then_inc(out_made, 1)

            def scores(t, b, step):
                dst = gath[b][:, :, FEAT:GROW].rearrange("p k h -> p h k")
                src = src_score[:, bass.ds(t, 1), :].rearrange("p o h -> p (o h)").unsqueeze(2).to_broadcast([ROWS, HEADS, SLOTS])
                step(V.tensor_tensor(score[:], dst, src, ALU.add))
                step(V.scalar_tensor_tensor(score[:], score[:], SLOPE, score[:], ALU.mult, ALU.max))

            def weigh(b, step, into):
                g = gath[b][:, :, 0:FEAT].rearrange("p k (h d) -> p k h d", h=HEADS)
                w = prob[:].rearrange("p h k -> p k h").unsqueeze(3).to_broadcast([ROWS, SLOTS, HEADS, HDIM])
                step(V.tensor_tensor(g, g, w, ALU.mult))
                return V.tensor_reduce(into[:], gath[b][:, :, 0:FEAT].rearrange("p k f -> p f k"), AX.X, ALU.add)

            with dve.If(bad_rows == 0):
                def stage_list(t, b, prior):
                    if prior is not None:
                        dve.wait_ge(attn_gathered[b], prior)
                    V.tensor_copy(stage[b][:], lists[:, bass.ds(t, 1), :].rearrange("p o k -> p (o k)")).then_inc(stage_ready, 1)

                def attend(t, u, b, prior):
                    step, count = stepper(dve, attn_step)
                    dve.wait_ge(attn_gathered[b], ALL * SLOTS * (u + 1))
                    scores(t, b, step)
                    step(V.tensor_reduce(peak[:], score[:], AX.X, ALU.max))
                    V.tensor_tensor(score[:], score[:], heads(peak), ALU.subtract).then_inc(score_made, 1)
                    dve.wait_ge(prob_made, t + 1)
                    V.tensor_reduce(total[:], prob[:], AX.X, ALU.add)
                    step_g = weigh(b, step, agg)
                    step_g.then_inc(attn_gath_free, 1)
                    dve.wait_ge(attn_gath_free, t + 1)
                    dve.wait_ge(mid_loaded[b], ALL * (u + 1))
                    finish(t, b, step, prior)

                for b in range(2):
                    stage_list(b, b, None)
                for b in range(2):
                    attend(b, 0, b, None)
                    stage_list(2 + b, b, ALL * SLOTS)

                def attn_turn(t, u, b):
                    attend(t, u, b, ALL * u)
                    stage_list(t + 2, b, ALL * SLOTS * (u + 1))
                pairs(dve, attn_turn, 2, TILES - 2)
                for b in range(2):
                    attend(TILES - 2 + b, TILES // 2 - 1, b, ALL * (TILES // 2 - 1))
            with dve.Else():
                mask = adj_in[0][:].bitcast(f32)
                dve.sem_inc(dense_free, 2)
                dve.sem_inc(dense_mask_free, 1)
                with dve.Fori(0, TILES) as t:
                    step, _ = stepper(dve, dense_step)
                    dve.wait_ge(dense_adj_loaded, ALL * (t + 1))
                    step(V.tensor_scalar(mask, adj_in[0][:], 0.0, None, ALU.not_equal))
                    step(V.memset(nb_max[:], 0.0))
                    with dve.Fori(0, BLOCKS // 2) as c2:
                        for b in range(2):
                            step, _ = stepper(dve, dense_step)
                            dve.wait_ge(dense_loaded[b], ALL * (t * (BLOCKS // 2) + c2 + 1))
                            g = gath[b][:, :, 0:FEAT]
                            m = mask[:, bass.ds((2 * c2 + b) * BLOCK, BLOCK)].unsqueeze(2).to_broadcast([ROWS, BLOCK, FEAT])
                            step(V.tensor_tensor(g, g, m, ALU.mult))
                            step(V.tensor_reduce(part[:], g.rearrange("p k f -> p f k"), AX.X, ALU.max))
                            step(V.tensor_tensor(nb_max[:], nb_max[:], part[:], ALU.max))
                            dve.sem_inc(dense_free, 1)
                    step, _ = stepper(dve, post_step)
                    dve.wait_ge(x_loaded[0], ALL * (TILES // 2 + t + 1))
                    post(t + TILES, 0, ALL * (TILES // 2) + ALL * t, step)
                    dve.sem_inc(dense_mask_free, 1)

                agg_h = agg[:].rearrange("p (h d) -> p h d", h=HEADS)
                with dve.Fori(0, TILES) as t:
                    step, _ = stepper(dve, dense_step)
                    dve.wait_ge(dense_adj_loaded, ALL * (t + 1 + TILES))
                    step(V.tensor_scalar(mask, adj_in[0][:], 0.0, None, ALU.is_gt))
                    step(V.memset(peak_new[:], -3.0e38))
                    step(V.memset(total[:], 0.0))
                    step(V.memset(agg[:], 0.0))
                    with dve.Fori(0, BLOCKS // 2) as c2:
                        for b in range(2):
                            step, _ = stepper(dve, dense_step)
                            n = t * BLOCKS + 2 * c2 + b
                            dve.wait_ge(dense_loaded[b], ALL * (t * (BLOCKS // 2) + c2 + 1 + TILES * (BLOCKS // 2)))
                            m1 = mask[:, bass.ds((2 * c2 + b) * BLOCK, BLOCK)]
                            scores(t, b, step)
                            step(V.tensor_tensor(score[:], score[:], m1.unsqueeze(1).to_broadcast([ROWS, HEADS, BLOCK]), ALU.mult))
                            step(V.tensor_scalar(is_nb[:], m1, -1.0, MASKED, ALU.add, ALU.mult))
                            step(V.tensor_tensor(score[:], score[:], is_nb[:].unsqueeze(1).to_broadcast([ROWS, HEADS, BLOCK]), ALU.add))
                            step(V.tensor_copy(peak[:], peak_new[:]))
                            step(V.tensor_reduce(part_sum[:], score[:], AX.X, ALU.max))
                            step(V.tensor_tensor(peak_new[:], peak[:], part_sum[:], ALU.max))
                            step(V.tensor_tensor(peak[:], peak[:], peak_new[:], ALU.subtract))
                            V.tensor_tensor(score[:], score[:], heads(peak_new), ALU.subtract).then_inc(dense_score, 1)
                            dve.wait_ge(dense_exp, n + 1)
                            step(V.tensor_reduce(part_sum[:], prob[:], AX.X, ALU.add))
                            step(V.tensor_tensor(total[:], total[:], rescale[:], ALU.mult))
                            step(weigh(b, step, part))
                            step(V.tensor_tensor(total[:], total[:], part_sum[:], ALU.add))
                            step(V.tensor_tensor(agg_h, agg_h, rescale[:].unsqueeze(2).to_broadcast([ROWS, HEADS, HDIM]), ALU.mult))
                            step(V.tensor_tensor(agg[:], agg[:], part[:], ALU.add))
                            dve.sem_inc(dense_free, 1)
                    dve.wait_ge(mid_loaded[0], ALL * (t + 1))
                    finish(t, 0, step, ALL * t)
                    dve.sem_inc(dense_mask_free, 1)


def kernel(x, adj, L1_gnn_W, L1_gnn_a):
    import numpy as np
    import concourse.bacc as bacc
    from concourse.bass_utils import run_bass_kernel_spmd

    arrays = {"x": np.asarray(x), "adj": np.asarray(adj), "weight": np.asarray(L1_gnn_W), "attn": np.asarray(L1_gnn_a)}
    nc = bacc.Bacc("TRN2", target_bir_lowering=False, num_devices=1)
    args = [nc.dram_tensor(n, a.shape, mybir.dt.from_np(a.dtype), kind="ExternalInput").ap() for n, a in arrays.items()]
    out = nc.dram_tensor("out", (NODES, FEAT), mybir.dt.float32, kind="ExternalOutput").ap()
    gnn_program(nc, *args, out)
    return run_bass_kernel_spmd(nc, [arrays], core_ids=[0]).results[0]["out"]
```

```python
from contextlib import ExitStack

import concourse.bass as bass
import concourse.mybir as mybir

NODES = 8192
FEAT = 128
HEADS = 4
HDIM = FEAT // HEADS
ROWS = 128
TILES = NODES // ROWS
CHUNK = 128
CHUNKS = NODES // CHUNK
SLOTS = 64
ROUNDS = SLOTS // 8
GROW = FEAT + HEADS
WINDOW = 8
PLACES = WINDOW * ROWS
LEAD = WINDOW + 2
COUNT, NODE, NODE1 = SLOTS, SLOTS + 1, SLOTS + 2
RECORD = SLOTS + 3
LEVELS = [*range(26, 46), 48, 52, 56, 60, 64]
DIGIT = 128
BLOCK = SLOTS
BLOCKS = NODES // BLOCK
EPS = 1e-5
SLOPE = 0.2
MASKED = 9.0e15
PAD_SCORE = -1.0e17
ALL = 16


def gnn_program(nc, x, adj, weight, attn, out):
    f32, bf16, i32, u32 = mybir.dt.float32, mybir.dt.bfloat16, mybir.dt.int32, mybir.dt.uint32
    ALU, ACT, AX = mybir.AluOpType, mybir.ActivationFunctionType, mybir.AxisListType

    node_table = nc.dram_tensor("node_table", (NODES + 1, FEAT), f32).ap()
    attn_table = nc.dram_tensor("attn_table", (NODES + 1, GROW), f32).ap()
    mid = nc.dram_tensor("mid", (NODES, FEAT), f32).ap()

    ctx = ExitStack()
    with ctx:
        def sb(name, shape, dt=f32):
            return ctx.enter_context(nc.sbuf_tensor(name, shape, dt))

        def ps(name, shape):
            return ctx.enter_context(nc.psum_tensor(name, shape, f32))

        def sem(name):
            return ctx.enter_context(nc.semaphore(name))

        adj_in = [sb(f"adj_in{b}", [ROWS, NODES], i32) for b in range(2)]
        keys = sb("keys", [ROWS, NODES], bf16)
        gath = [sb(f"gath{b}", [ROWS, SLOTS, GROW]) for b in range(2)]
        records = sb("records", [ROWS, TILES, RECORD], u32)
        stage = [sb(f"stage{s}", [ROWS, RECORD], u32) for s in range(4)]
        built = sb("built", [ROWS, WINDOW, RECORD])
        node_number = sb("node_number", [ROWS, TILES, 2])
        tie = sb("tie", [ROWS, WINDOW])
        sort_key = sb("sort_key", [ROWS, WINDOW])
        int_space = [sb(f"int_space{d}", [ROWS, max(CHUNKS * 8, WINDOW * RECORD)], u32) for d in range(2)]
        built_int, digit_int = (v[:, 0:WINDOW * RECORD].rearrange("p (k r) -> p k r", r=RECORD) for v in int_space)
        cand, cand_base = (v[:, 0:CHUNKS * 8].bitcast(f32).rearrange("p (c k) -> p c k", k=8) for v in int_space)
        digits = [sb(f"digits{d}", [ROWS, WINDOW, RECORD], bf16) for d in range(2)]
        standing = sb("standing", [ROWS, WINDOW])
        place_number = sb("place_number", [ROWS, PLACES], mybir.dt.int16)
        onehot = sb("onehot", [ROWS, WINDOW, PLACES], bf16)
        key_diag = onehot[:, 0:2, :].rearrange("p k n -> p (k n)").bitcast(f32).rearrange("p (k r) -> p k r", r=ROWS)
        column_number = sb("column_number", [ROWS, CHUNK], bf16)
        chunk_base = sb("chunk_base", [ROWS, CHUNKS])
        is_nb = sb("is_nb", [ROWS, SLOTS])
        square_sum = sb("square_sum", [ROWS, TILES])
        listed = sb("listed", [ROWS, TILES])
        x_t = [sb(f"x_t{b}", [ROWS, FEAT]) for b in range(2)]
        mid_t = [sb(f"mid_t{b}", [ROWS, FEAT]) for b in range(2)]
        row_t = [sb(f"row_t{b}", [ROWS, GROW]) for b in range(2)]
        src_score = sb("src_score", [ROWS, TILES, HEADS])
        nb_max = sb("nb_max", [ROWS, FEAT])
        bn = sb("bn", [ROWS, 6])
        mean_var = sb("mean_var", [ROWS, 2])
        std = sb("std", [ROWS, 1])
        rstd = sb("rstd", [ROWS, 1])
        shift = sb("shift", [ROWS, 1])
        normed = sb("normed", [ROWS, FEAT])
        normed_T = sb("normed_T", [FEAT, ROWS])
        sums, neg_mean, var_sums, shifts = (sb(name, [ROWS, TILES]) for name in ("sums", "neg_mean", "var_sums", "shifts"))
        stat_r = sb("stat_r", [ROWS, TILES])
        eps_t = sb("eps_t", [ROWS, 1])
        quarter = sb("quarter", [ROWS, 1])
        ones = sb("ones", [ROWS, ROWS])
        ident = sb("ident", [ROWS, ROWS])
        w_cat = sb("w_cat", [FEAT, FEAT + 2 * HEADS])
        w_T = sb("w_T", [FEAT, FEAT])
        a_blocks = sb("a_blocks", [FEAT, 2 * HEADS])
        pad_row = sb("pad_row", [1, GROW])
        score = sb("score", [ROWS, HEADS, SLOTS])
        prob = sb("prob", [ROWS, HEADS, SLOTS])
        peak = sb("peak", [ROWS, HEADS])
        total = sb("total", [ROWS, HEADS])
        agg = sb("agg", [ROWS, FEAT])
        neg = sb("neg", [ROWS, FEAT])
        neg_exp = sb("neg_exp", [ROWS, FEAT])
        pos = sb("pos", [ROWS, FEAT])
        out_t = [sb(f"out_t{b}", [ROWS, FEAT]) for b in range(2)]
        bad = sb("bad", [ROWS, TILES])
        empty = sb("empty", [ROWS, TILES])
        bad_row = sb("bad_row", [ROWS, 1])
        bad_count = sb("bad_count", [1, 1], i32)
        peak_new = sb("peak_new", [ROWS, HEADS])
        rescale = sb("rescale", [ROWS, HEADS])
        part = pos
        part_sum = sb("part_sum", [ROWS, HEADS])

        p_keys = ps("p_keys", [ROWS, PLACES])
        p_sorted = ps("p_sorted", [ROWS, WINDOW, ROWS])
        p_T = ps("p_T", [FEAT, ROWS])
        p_row = ps("p_row", [ROWS, FEAT + 2 * HEADS])
        p_w = ps("p_w", [FEAT, FEAT])
        p_small = ps("p_small", [FEAT, 2 * HEADS + 1])
        p_a = p_small[:, 0:2 * HEADS]
        p_bad = p_small[0:1, 2 * HEADS:]

        weights_loaded = sem("weights_loaded")
        a_zeroed = sem("a_zeroed")
        a_loaded = sem("a_loaded")
        all_x_loaded = sem("all_x_loaded")
        const_made = sem("const_made")
        pad_made = sem("pad_made")
        setup = sem("setup")
        var_made = sem("var_made")
        std_made = sem("std_made")
        sums_made = sem("sums_made")
        neg_mean_made = sem("neg_mean_made")
        shifts_made = sem("shifts_made")
        nodes_relued = sem("nodes_relued")
        nodes_stored = sem("nodes_stored")
        wT_done = sem("wT_done")
        wT_copied = sem("wT_copied")
        wa_done = sem("wa_done")
        w_ready = sem("w_ready")
        adj_loaded = [sem(f"adj_loaded{b}") for b in range(2)]
        cast_done = sem("cast_done")
        squares_done = sem("squares_done")
        keys_used = sem("keys_used")
        build_step = sem("build_step")
        diag_made = sem("diag_made")
        keys_spread = sem("keys_spread")
        onehots_made = sem("onehots_made")
        standing_made = sem("standing_made")
        squares_made = sem("squares_made")
        digits_made = sem("digits_made")
        sorted_done = sem("sorted_done")
        records_made = sem("records_made")
        list_ready = sem("list_ready")
        dve_holds = sem("dve_holds")
        gathered = [sem(f"gathered{b}") for b in range(2)]
        buffers_free = sem("buffers_free")
        max_made = sem("max_made")
        pool_holds = sem("pool_holds")
        post_step = sem("post_step")
        tile_var = sem("tile_var")
        tile_std = sem("tile_std")
        shift_made = sem("shift_made")
        mid_made = sem("mid_made")
        tile_normed = sem("tile_normed")
        transposed = sem("transposed")
        T_copied = sem("T_copied")
        projected = sem("projected")
        row_made = sem("row_made")
        scattered = [sem(f"scattered{b}") for b in range(2)]
        mid_stored = [sem(f"mid_stored{b}") for b in range(2)]
        check_step = sem("check_step")
        bad_row_made = sem("bad_row_made")
        bad_summed = sem("bad_summed")
        verdict = sem("verdict")
        stage_ready = sem("stage_ready")
        attn_gathered = [sem(f"attn_gathered{b}") for b in range(2)]
        attn_buffers_free = sem("attn_buffers_free")
        agg_made = sem("agg_made")
        out_ready = sem("out_ready")
        attn_step = sem("attn_step")
        score_made = sem("score_made")
        prob_made = sem("prob_made")
        neg_made = sem("neg_made")
        neg_exped = sem("neg_exped")
        mid_loaded = [sem(f"mid_loaded{b}") for b in range(2)]
        out_made = sem("out_made")
        dense_out_stored = sem("dense_out_stored")
        dense_x_loaded = sem("dense_x_loaded")
        dense_row_stored = sem("dense_row_stored")
        dense_adj_loaded = sem("dense_adj_loaded")
        dense_mask_free = sem("dense_mask_free")
        dense_loaded = [sem(f"dense_loaded{b}") for b in range(2)]
        dense_free = sem("dense_free")
        dense_step = sem("dense_step")
        dense_score = sem("dense_score")
        dense_exp = sem("dense_exp")

        block = ctx.enter_context(nc.Block())

        adj_rows = adj.rearrange("(t p) n -> t p n", p=ROWS)
        x_rows = x.rearrange("(t p) f -> t p f", p=ROWS)
        mid_rows = mid.rearrange("(t p) f -> t p f", p=ROWS)
        out_rows = out.rearrange("(t p) f -> t p f", p=ROWS)
        attn_rows = attn_table[1:NODES + 1, :].rearrange("(t p) f -> t p f", p=ROWS)
        node_blocks = node_table[1:NODES + 1, :].rearrange("(c k) f -> c k f", k=BLOCK)
        attn_blocks = attn_table[1:NODES + 1, :].rearrange("(c k) f -> c k f", k=BLOCK)
        all_x = gath[0][:, 0:TILES, 0:FEAT]
        all_sq = gath[1][:, 0:TILES, 0:FEAT]

        class Tile:

            def __init__(self, v, j):
                self.v, self.j = v, j
                self.number = WINDOW * v + j
                self.half = (WINDOW // 2) * v + j // 2
                self.b, self.s, self.k = j % 2, j % 4, j % WINDOW
                self.window = v + j // WINDOW

            def plus(self, d):
                return Tile(self.v, self.j + d)

        def tile_of(rows, t):
            return rows[bass.ds(t, 1), :, :].rearrange("o p f -> (o p) f")

        def column(tensor, t):
            return tensor[:, bass.ds(t, 1), :].rearrange("p o c -> p (o c)")

        def stepper(engine, semaphore):
            count = [0]
            engine.sem_clear(semaphore)

            def step(ins):
                count[0] += 1
                ins.then_inc(semaphore, 1)
                engine.wait_ge(semaphore, count[0])
            return step

        def steps(engine, body):
            for j in range(LEAD):
                body(Tile(0, j), None)
            turns = (TILES - 2 * WINDOW) // WINDOW
            with engine.Fori(0, turns) as v:
                for j in range(WINDOW):
                    body(Tile(v, j + LEAD), Tile(v, j))
            for j in range(turns * WINDOW, TILES):
                body(Tile(0, j + LEAD) if j + LEAD < TILES else None, Tile(0, j))

        def sorted_tiles(engine, body, per_turn=WINDOW):
            with engine.Fori(0, TILES // WINDOW - 1) as v:
                for j in range(WINDOW):
                    body(Tile(v, j))
            for j in range(TILES - WINDOW, TILES):
                body(Tile(0, j))

        def level_of(slot):
            return max([level for level in LEVELS if level <= slot], default=0)

        def by_level(engine, length, levels, body):
            if len(levels) == 1:
                body(levels[0])
                return
            mid_level = len(levels) // 2
            with engine.If(length <= levels[mid_level - 1]):
                by_level(engine, length, levels[:mid_level], body)
            with engine.Else():
                by_level(engine, length, levels[mid_level:], body)

        def longest(engine, s):
            return engine.value_load(stage[s][0:1, COUNT:COUNT + 1], min_val=0, max_val=SLOTS)

        @block.sync
        def _(sp):
            sp.sem_inc(squares_done, 2)

            def load_adj(n):
                sp.wait_ge(squares_done, n.number + 1)
                sp.dma_start(adj_in[n.b][:], tile_of(adj_rows, n.number)).then_inc(adj_loaded[n.b], ALL)

            load_adj(Tile(0, 0))
            sp.dma_start(all_x, x.rearrange("(t p) f -> p t f", p=ROWS)).then_inc(all_x_loaded, ALL)
            load_adj(Tile(0, 1))
            sp.dma_start(w_cat[:, 0:FEAT], weight).then_inc(weights_loaded, ALL)
            sp.wait_ge(a_zeroed, 1)
            for h in range(HEADS):
                for col, lo in ((h, HDIM), (HEADS + h, 0)):
                    sp.dma_start(a_blocks[h * HDIM:(h + 1) * HDIM, col:col + 1],
                                 attn[0, h, lo:lo + HDIM].unsqueeze(1)).then_inc(a_loaded, ALL)


            def turn(n, q):
                if n is not None and not (isinstance(n.v, int) and n.number + 2 >= TILES):
                    load_adj(n.plus(2))
                if q is None and n.number == 5:
                    sp.wait_ge(nodes_relued, TILES // 4)
                    sp.dma_start(node_table[1:NODES + 1, :].rearrange("(t p) f -> p t f", p=ROWS), all_x).then_inc(nodes_stored, ALL)
                if q is not None:
                    sp.wait_ge(mid_made, q.number + 1)
                    sp.dma_start(tile_of(mid_rows, q.number), mid_t[q.b][:]).then_inc(mid_stored[q.b], ALL)
            steps(sp, turn)

            for b in range(2):
                sp.wait_ge(mid_stored[b], ALL * (1 + TILES // 2))
            sp.wait_ge(verdict, 1)
            bad_rows = sp.value_load(bad_count[0:1, 0:1], min_val=0, max_val=ROWS)
            with sp.If(bad_rows == 0):
                sp.sem_inc(out_made, 2)

                def load_mid(q):
                    sp.wait_ge(out_made, q.number + 1)
                    sp.dma_start(mid_t[q.b][:], tile_of(mid_rows, q.number)).then_inc(mid_loaded[q.b], ALL)
                sorted_tiles(sp, load_mid)
            with sp.Else():
                def dense_blocks(t_all, rows_of, width):
                    with sp.Fori(0, BLOCKS // 2) as c2:
                        for b in range(2):
                            n = t_all * BLOCKS + 2 * c2 + b
                            sp.wait_ge(dense_free, n + 1)
                            src = rows_of[bass.ds(2 * c2 + b, 1), :, :].rearrange("o k f -> (o k) f")
                            sp.dma_start(gath[b][:, :, 0:width], src.unsqueeze(0).to_broadcast([ROWS, BLOCK, width])).then_inc(dense_loaded[b], ALL)

                for b in range(2):
                    sp.wait_ge(scattered[b], ALL * (1 + TILES // 2))
                with sp.Fori(0, TILES) as t:
                    sp.wait_ge(dense_mask_free, t + 1)
                    sp.dma_start(adj_in[0][:], tile_of(adj_rows, t)).then_inc(dense_adj_loaded, ALL)
                    sp.dma_start(x_t[0][:], tile_of(x_rows, t)).then_inc(dense_x_loaded, ALL)
                    dense_blocks(t, node_blocks, FEAT)
                    sp.wait_ge(mid_made, t + TILES + 1)
                    sp.dma_start(tile_of(mid_rows, t), mid_t[0][:]).then_inc(mid_stored[0], ALL)
                    sp.wait_ge(row_made, t + TILES + 1)
                    sp.dma_start(tile_of(attn_rows, t), row_t[0][:]).then_inc(dense_row_stored, ALL)
                sp.wait_ge(mid_stored[0], ALL * (1 + TILES // 2 + TILES))
                sp.wait_ge(dense_row_stored, ALL * (1 + TILES))
                with sp.Fori(0, TILES) as t:
                    sp.wait_ge(dense_mask_free, t + TILES + 1)
                    sp.dma_start(adj_in[0][:], tile_of(adj_rows, t)).then_inc(dense_adj_loaded, ALL)
                    sp.dma_start(mid_t[0][:], tile_of(mid_rows, t)).then_inc(mid_loaded[0], ALL)
                    dense_blocks(t + TILES, attn_blocks, GROW)
                    sp.wait_ge(out_made, t + 1)
                    sp.dma_start(tile_of(out_rows, t), out_t[0][:]).then_inc(dense_out_stored, ALL)
                sp.wait_ge(dense_out_stored, ALL * (1 + TILES))

        @block.gpsimd
        def _(pool):
            pool.memset(a_blocks[:], 0.0).then_inc(a_zeroed, 1)

            def numbers(tensor, pattern, base, step):
                pool.iota(tensor, pattern=pattern, base=base, channel_multiplier=step,
                          allow_small_or_imprecise_dtypes=True).then_inc(const_made, 1)
            numbers(column_number[:], [[1, CHUNK]], 1, 0)
            numbers(chunk_base[:], [[CHUNK, CHUNKS]], 0, 0)
            numbers(node_number[:], [[ROWS, TILES], [1, 2]], 0, 1)
            numbers(place_number[:], [[2, PLACES]], 1 - PLACES, 0)
            numbers(tie[:], [[ROWS, WINDOW]], 0, 1)
            pool.memset(ident[:], 0.0).then_inc(const_made, 1)
            pool.wait_ge(const_made, 6)
            pool.affine_select(out=ident[:], in_=ident[:], compare_op=ALU.not_equal, fill=1.0, base=0,
                               pattern=[[-1, ROWS]], channel_multiplier=1).then_inc(const_made, 1)
            pool.memset(eps_t[:], EPS).then_inc(const_made, 1)
            pool.memset(quarter[:], -0.25).then_inc(const_made, 1)
            pool.memset(ones[:], 1.0).then_inc(const_made, 1)
            pool.memset(pad_row[:, 0:FEAT], 0.0).then_inc(pad_made, 1)
            pool.memset(pad_row[:, FEAT:GROW], PAD_SCORE).then_inc(pad_made, 1)
            pool.wait_ge(pad_made, 2)
            pool.dma_start(node_table[0:1, :], pad_row[:, 0:FEAT]).then_inc(scattered[0], ALL)
            pool.dma_start(attn_table[0:1, :], pad_row[:, :]).then_inc(scattered[1], ALL)
            pool.wait_ge(nodes_stored, ALL)
            for b in range(2):
                pool.wait_ge(scattered[b], ALL)

            def gather_row(dst, table, s, col, done):
                pool.indirect_dma_start(dst, None, table, bass.IndirectOffsetOnAxis(ap=stage[s][:, col:col + 1], axis=0)).then_inc(done, ALL)

            def gather(table, width, q, done):
                def slots_from(first):
                    if first == SLOTS:
                        return
                    with pool.If(length > level_of(first)):
                        end = min(first + 8, SLOTS)
                        for k in range(first, end):
                            if level_of(k) == level_of(first):
                                gather_row(gath[q.b][:, k, 0:width], table, q.s, k, done)
                                continue
                            with pool.If(length > level_of(k)):
                                gather_row(gath[q.b][:, k, 0:width], table, q.s, k, done)
                            with pool.Else():
                                pool.nop()
                        slots_from(end)
                    with pool.Else():
                        pool.nop()
                for k in range(LEVELS[0]):
                    gather_row(gath[q.b][:, k, 0:width], table, q.s, k, done)
                length = longest(pool, q.s)
                slots_from(LEVELS[0])

            def gather_max(q):
                pool.wait_ge(buffers_free, q.number + 1)
                pool.sem_inc(pool_holds, 1)
                pool.wait_ge(list_ready, q.number + 1)
                pool.sem_inc(pool_holds, 1)
                gather_row(x_t[q.b][:], x, q.s, NODE, gathered[q.b])
                gather(node_table, FEAT, q, gathered[q.b])

            def scatter_row(q):
                pool.wait_ge(row_made, q.number + 1)
                pool.sem_inc(pool_holds, 1)
                pool.indirect_dma_start(attn_table, bass.IndirectOffsetOnAxis(ap=stage[q.s][:, NODE1:NODE1 + 1], axis=0),
                                        row_t[q.b][:], None).then_inc(scattered[q.b], ALL)

            def turn(q):
                if not (isinstance(q.v, int) and q.number == TILES - 1):
                    gather_max(q.plus(1))
                scatter_row(q)
            gather_max(Tile(0, 0))
            sorted_tiles(pool, turn)

            pool.wait_ge(verdict, 1)
            bad_rows = pool.value_load(bad_count[0:1, 0:1], min_val=0, max_val=ROWS)
            with pool.If(bad_rows == 0):
                for b in range(2):
                    pool.wait_ge(scattered[b], ALL * (1 + TILES // 2))

                def gather_attn(q):
                    pool.wait_ge(attn_buffers_free, q.number + 1)
                    pool.sem_inc(pool_holds, 1)
                    pool.wait_ge(stage_ready, q.number + 1)
                    pool.sem_inc(pool_holds, 1)
                    gather(attn_table, GROW, q, attn_gathered[q.b])

                def scatter_out(q):
                    pool.wait_ge(out_ready, q.number + 1)
                    pool.sem_inc(pool_holds, 1)
                    pool.indirect_dma_start(out, bass.IndirectOffsetOnAxis(ap=stage[q.s][:, NODE:NODE + 1], axis=0),
                                            out_t[q.b][:], None).then_inc(scattered[q.b], ALL)

                def attn_turn(q):
                    if not (isinstance(q.v, int) and q.number == TILES - 1):
                        gather_attn(q.plus(1))
                    scatter_out(q)
                gather_attn(Tile(0, 0))
                sorted_tiles(pool, attn_turn)
                for b in range(2):
                    pool.wait_ge(scattered[b], ALL * (1 + TILES))
            with pool.Else():
                pool.nop()

        @block.tensor
        def _(pe):
            pe.wait_ge(const_made, 10)
            pe.wait_ge(weights_loaded, ALL)
            nc.tensor.transpose(p_w[:], w_cat[:, 0:FEAT], ident[:]).then_inc(wT_done, 1)
            pe.wait_ge(wT_copied, 1)
            pe.wait_ge(a_loaded, ALL * 2 * HEADS)
            nc.tensor.matmul(p_a, w_T[:], a_blocks[:], start=True, stop=True).then_inc(wa_done, 1)
            pe.wait_ge(w_ready, 1)

            def spread_keys(w):
                pe.wait_ge(diag_made, w + 1)
                diag = key_diag.rearrange("p k r -> p (k r)")
                for c in range(0, PLACES, 512):
                    last = nc.tensor.matmul(p_keys[:, c:c + 512], ones[:], diag[:, c:c + 512], start=True, stop=True)
                last.then_inc(keys_spread, 1)

            def sort_window(w):
                pe.wait_ge(records_made, w + 1)
                pe.wait_ge(digits_made, w + 1)
                pe.wait_ge(onehots_made, w + 1)
                terms = [(k, d) for k in range(WINDOW) for d in range(2)]
                for q in range(WINDOW):
                    for k, d in terms:
                        last = nc.tensor.matmul(p_sorted[:, q, 0:RECORD], onehot[:, k, q * ROWS:(q + 1) * ROWS],
                                                digits[d][:, k, :], start=(k, d) == terms[0], stop=(k, d) == terms[-1])
                last.then_inc(sorted_done, 1)

            def project(s):
                pe.wait_ge(tile_normed, s + 1)
                nc.tensor.transpose(p_T[:], normed[:], ident[:]).then_inc(transposed, 1)
                pe.wait_ge(T_copied, s + 1)
                nc.tensor.matmul(p_row[:], normed_T[:], w_cat[:], start=True, stop=True).then_inc(projected, 1)

            def turn(n, q):
                window_built = n is not None and n.k == WINDOW - 1
                if window_built:
                    spread_keys(n.window)
                if q is not None:
                    project(q.number)
                if window_built:
                    sort_window(n.window)
            steps(pe, turn)
            pe.wait_ge(bad_row_made, 1)
            nc.tensor.matmul(p_bad, bad_row[:], ones[:, 0:1], start=True, stop=True).then_inc(bad_summed, 1)
            pe.wait_ge(verdict, 1)
            bad_rows = pe.value_load(bad_count[0:1, 0:1], min_val=0, max_val=ROWS)
            with pe.If(bad_rows == 0):
                pe.nop()
            with pe.Else():
                with pe.Fori(0, TILES) as t:
                    project(t + TILES)

        @block.scalar
        def _(act):
            act.sem_inc(keys_used, 1)
            act.sem_inc(records_made, 1)
            act.wait_ge(const_made, 10)

            def over_tiles(body, done):
                with act.Fori(0, TILES // 4) as v:
                    for j in range(4):
                        last = body(4 * v + j)
                    last.then_inc(done, 1)

            def input_sums():
                act.wait_ge(all_x_loaded, ALL)
                over_tiles(lambda t: nc.scalar.activation(column(all_sq, t), column(all_x, t), ACT.Copy,
                                                          accum_out=sums[:, bass.ds(t, 1)]), sums_made)

            def input_variances():
                act.wait_ge(neg_mean_made, 1)
                over_tiles(lambda t: nc.scalar.activation(column(all_sq, t), column(all_x, t), ACT.Square, bias=neg_mean[:, bass.ds(t, 1)],
                                                          accum_out=var_sums[:, bass.ds(t, 1)]), var_made)
                act.wait_ge(var_made, TILES // 4)
                nc.scalar.activation(stat_r[:], var_sums[:], ACT.Sqrt, bias=eps_t[:], scale=1.0 / FEAT).then_inc(std_made, 1)

            def input_normed():
                act.wait_ge(shifts_made, 1)
                over_tiles(lambda t: nc.scalar.activation(column(all_x, t), column(all_x, t), ACT.Relu, bias=shifts[:, bass.ds(t, 1)],
                                                          scale=stat_r[:, bass.ds(t, 1)]), nodes_relued)

            def cast(n):
                act.wait_ge(adj_loaded[n.b], ALL * (n.half + 1))
                act.wait_ge(keys_used, n.number + 1)
                nc.scalar.activation(keys[:], adj_in[n.b][:], ACT.Copy).then_inc(cast_done, 1)

            def square(n):
                act.wait_ge(cast_done, n.number + 1)
                nc.scalar.activation(adj_in[n.b][:].bitcast(f32), adj_in[n.b][:], ACT.Square, bias=quarter[:],
                                     accum_out=square_sum[:, bass.ds(n.number, 1)]).then_inc(squares_done, 1)

            def sort_places(w):
                act.wait_ge(keys_spread, w + 1)
                for k in range(WINDOW):
                    last = nc.scalar.activation(onehot[:, k, :], p_keys[:], ACT.Sign, scale=-1.0, bias=sort_key[:, k:k + 1],
                                                accum_out=standing[:, k:k + 1])
                last.then_inc(standing_made, 1)
                act.wait_ge(standing_made, w + 1)
                for k in range(WINDOW):
                    last = nc.scalar.activation(onehot[:, k, :], place_number[:], ACT.Square, bias=standing[:, k:k + 1])
                last.then_inc(squares_made, 1)
                act.wait_ge(squares_made, w + 1)
                nc.scalar.activation(onehot[:], onehot[:], ACT.Relu, scale=-1.0, bias=ones[:, 0:1]).then_inc(onehots_made, 1)

            def take_records(w):
                act.wait_ge(sorted_done, w + 2)
                nc.scalar.activation(records[:, bass.ds(w * WINDOW, WINDOW), :], p_sorted[:, :, 0:RECORD],
                                     ACT.Copy).then_inc(records_made, 1)

            def norm_and_row(t, s, b, stored, value):
                act.wait_ge(tile_var, s + 1)
                nc.scalar.activation(std[:], mean_var[:, 1:2], ACT.Sqrt, bias=eps_t[:]).then_inc(tile_std, 1)
                act.wait_ge(shift_made, s + 1)
                nc.scalar.activation(normed[:], mid_t[b][:], ACT.Relu, bias=shift[:], scale=rstd[:]).then_inc(tile_normed, 1)
                act.wait_ge(transposed, s + 1)
                nc.scalar.activation(normed_T[:], p_T[:], ACT.Copy).then_inc(T_copied, 1)
                act.wait_ge(projected, s + 1)
                act.wait_ge(stored, value)
                nc.scalar.activation(row_t[b][:], p_row[:, 0:GROW], ACT.Copy)
                nc.scalar.activation(column(src_score, t), p_row[:, GROW:], ACT.Copy).then_inc(row_made, 1)

            def join_weights():
                act.wait_ge(wT_done, 1)
                nc.scalar.activation(w_T[:], p_w[:], ACT.Copy).then_inc(wT_copied, 1)
                act.wait_ge(wa_done, 1)
                act.wait_ge(weights_loaded, ALL)
                nc.scalar.activation(w_cat[:, FEAT:], p_a, ACT.Copy).then_inc(w_ready, 1)

            cast(Tile(0, 0))
            square(Tile(0, 0))
            meanwhile = {0: input_sums, 2: input_variances, 4: input_normed, 6: join_weights}

            def turn(n, q):
                more = n is not None and not (isinstance(n.v, int) and n.number + 1 >= TILES)
                if more:
                    cast(n.plus(1))
                if q is None and n.number in meanwhile:
                    meanwhile[n.number]()
                if q is not None:
                    norm_and_row(q.number, q.number, q.b, scattered[q.b], ALL * (q.half + 1))
                if n is not None and n.k == WINDOW - 1:
                    sort_places(n.window)
                if more:
                    square(n.plus(1))
                if n is not None and n.k == WINDOW - 1:
                    take_records(n.window)
            steps(act, turn)

            act.wait_ge(verdict, 1)
            bad_rows = act.value_load(bad_count[0:1, 0:1], min_val=0, max_val=ROWS)

            def elu_exp(t):
                act.wait_ge(neg_made, t + 1)
                nc.scalar.activation(neg_exp[:], neg[:], ACT.Exp).then_inc(neg_exped, 1)

            with act.If(bad_rows == 0):
                with act.Fori(0, TILES) as t:
                    act.wait_ge(score_made, t + 1)
                    nc.scalar.activation(prob[:], score[:], ACT.Exp).then_inc(prob_made, 1)
                    elu_exp(t)
            with act.Else():
                act.sem_inc(dense_row_stored, ALL)
                for b in range(2):
                    act.wait_ge(scattered[b], ALL * (1 + TILES // 2))
                with act.Fori(0, TILES) as t:
                    norm_and_row(t, t + TILES, 0, dense_row_stored, ALL * (t + 1))
                with act.Fori(0, TILES) as t:
                    with act.Fori(0, BLOCKS) as c:
                        act.wait_ge(dense_score, t * BLOCKS + c + 1)
                        nc.scalar.activation(prob[:], score[:], ACT.Exp)
                        nc.scalar.activation(rescale[:], peak[:], ACT.Exp).then_inc(dense_exp, 1)
                    elu_exp(t)

        @block.vector
        def _(dve):
            V = nc.vector
            dve.sem_inc(buffers_free, 2)
            dve.sem_inc(sorted_done, 1)
            for b in range(2):
                dve.sem_inc(mid_stored[b], ALL)
            step = stepper(dve, setup)
            step(V.memset(score[:], 0.0))
            dve.wait_ge(const_made, 10)

            def input_means():
                dve.wait_ge(sums_made, TILES // 4)
                V.tensor_scalar(neg_mean[:], sums[:], -1.0 / FEAT, None, ALU.mult).then_inc(neg_mean_made, 1)

            def input_shifts():
                step = stepper(dve, setup)
                dve.wait_ge(std_made, 1)
                step(V.reciprocal(stat_r[:], stat_r[:]))
                V.tensor_tensor(shifts[:], neg_mean[:], stat_r[:], ALU.mult).then_inc(shifts_made, 1)

            def build(n):
                step = stepper(dve, build_step)
                dve.wait_ge(cast_done, n.number + 1)
                by_chunk = keys[:].rearrange("p (c n) -> p c n", n=CHUNK)
                step(V.tensor_tensor(by_chunk, by_chunk,
                                     column_number[:].unsqueeze(1).to_broadcast([ROWS, CHUNKS, CHUNK]), ALU.mult))
                for c in range(CHUNKS):
                    last = V.max(cand[:, c, :], by_chunk[:, c, :])
                last.then_inc(keys_used, 1)
                dve.wait_ge(keys_used, n.number + 2)
                base_b = chunk_base[:].unsqueeze(2).to_broadcast([ROWS, CHUNKS, 8])
                step(V.scalar_tensor_tensor(cand_base, cand, 0.0, base_b, ALU.is_gt, ALU.mult))
                step(V.tensor_tensor(cand, cand, cand_base, ALU.add))
                flat = cand.rearrange("p c k -> p (c k)")
                for r in range(ROUNDS):
                    eight = built[:, n.k, 8 * r:8 * r + 8]
                    step(V.max(eight, flat))
                    if r < ROUNDS - 1:
                        step(V.match_replace(flat, eight, flat, 0.0))
                step(V.tensor_scalar(is_nb[:], built[:, n.k, 0:SLOTS], 0.0, 0.0, ALU.is_gt, ALU.add,
                                     accum_out=built[:, n.k, COUNT:COUNT + 1]))

            def rank_window(w):
                step = stepper(dve, build_step)
                first = w * WINDOW
                V.tensor_copy(listed[:, bass.ds(first, WINDOW)], built[:, :, COUNT])
                V.tensor_copy(built[:, :, NODE:NODE1 + 1], node_number[:, bass.ds(first, WINDOW), :])
                step(V.scalar_tensor_tensor(sort_key[:], built[:, :, COUNT], float(PLACES), tie[:], ALU.mult, ALU.add))
                dve.wait_ge(sorted_done, w + 1)
                V.tensor_tensor(key_diag, ident[:].unsqueeze(1).to_broadcast([ROWS, WINDOW, ROWS]),
                                sort_key[:].unsqueeze(2).to_broadcast([ROWS, WINDOW, ROWS]), ALU.mult).then_inc(diag_made, 1)
                step(V.tensor_copy(built_int, built[:]))
                for d, bits in enumerate((NODES * 2 - DIGIT, DIGIT - 1)):
                    step(V.tensor_scalar(digit_int, built_int, bits, None, ALU.bitwise_and))
                    step(V.tensor_copy(digits[d][:], digit_int))
                dve.sem_inc(digits_made, 1)

            def stage_record(q):
                dve.wait_ge(records_made, q.window + 2)
                if not (isinstance(q.v, int) and q.number < 4):
                    dve.wait_ge(scattered[q.b], ALL * q.half)
                V.tensor_copy(stage[q.s][:], column(records, q.number)).then_inc(list_ready, 1)

            def post(s, b, stored_before, step):
                dve.wait_ge(mid_stored[b], stored_before)
                V.tensor_tensor(mid_t[b][:], x_t[b][:], nb_max[:], ALU.add).then_inc(mid_made, 1)
                dve.wait_ge(mid_made, s + 1)
                step(V.bn_stats(bn[:], mid_t[b][:]))
                V.bn_aggr(mean_var[:], bn[:]).then_inc(tile_var, 1)
                dve.wait_ge(tile_std, s + 1)
                step(V.reciprocal(rstd[:], std[:]))
                V.scalar_tensor_tensor(shift[:], mean_var[:, 0:1], -1.0, rstd[:], ALU.mult, ALU.mult).then_inc(shift_made, 1)

            expected = [dve.alloc_register(f"expected{b}") for b in range(2)]
            for b in range(2):
                dve.reg_mov(expected[b], 0)

            def landed(b, done, dmas):
                dve.reg_add(expected[b], expected[b], ALL * dmas)
                dve.wait_ge(done, dve.snap(expected[b]))
                dve.sem_inc(dve_holds, 1)

            def maximum(q):
                step = stepper(dve, post_step)
                dve.wait_ge(list_ready, q.number + 1)
                dve.sem_inc(dve_holds, 1)
                length = longest(dve, q.s)

                def with_slots(slots):
                    landed(q.b, gathered[q.b], slots + 1)
                    V.tensor_reduce(nb_max[:], gath[q.b][:, 0:slots, 0:FEAT].rearrange("p k f -> p f k"),
                                    AX.X, ALU.max).then_inc(max_made, 1)
                by_level(dve, length, LEVELS, with_slots)
                dve.wait_ge(max_made, q.number + 1)
                post(q.number, q.b, ALL * (q.half + 1), step)
                dve.wait_ge(mid_made, q.number + 1)
                dve.sem_inc(buffers_free, 1)

            def turn(n, q):
                if n is not None:
                    build(n)
                    if n.k == WINDOW - 1:
                        rank_window(n.window)
                if q is None:
                    if n.number == 1:
                        input_means()
                    if n.number == 3:
                        input_shifts()
                    if n.number == WINDOW:
                        for j in range(2):
                            stage_record(Tile(0, j))
                    return
                maximum(q)
                if not (isinstance(q.v, int) and q.number + 2 >= TILES):
                    stage_record(q.plus(2))
            steps(dve, turn)

            step = stepper(dve, check_step)
            dve.wait_ge(squares_done, TILES + 2)
            step(V.tensor_scalar(bad[:], listed[:], 0.5, NODES / 16, ALU.mult, ALU.add))
            step(V.tensor_tensor(bad[:], bad[:], square_sum[:], ALU.not_equal))
            step(V.tensor_scalar(empty[:], listed[:], 0.0, None, ALU.is_equal))
            step(V.tensor_tensor(bad[:], bad[:], empty[:], ALU.max))
            step(V.tensor_reduce(bad_row[:], bad[:], AX.X, ALU.max))
            dve.sem_inc(bad_row_made, 1)
            dve.wait_ge(bad_summed, 1)
            V.tensor_copy(bad_count[:], p_bad).then_inc(verdict, 1)
            dve.wait_ge(verdict, 1)
            bad_rows = dve.value_load(bad_count[0:1, 0:1], min_val=0, max_val=ROWS)

            def finish(t, b, step, stored, value):
                step(V.reciprocal(total[:], total[:]))
                agg_h = agg[:].rearrange("p (h d) -> p h d", h=HEADS)
                step(V.tensor_tensor(agg_h, agg_h, total[:].unsqueeze(2).to_broadcast([ROWS, HEADS, HDIM]), ALU.mult))
                V.tensor_scalar(neg[:], agg[:], 0.0, None, ALU.min).then_inc(neg_made, 1)
                step(V.scalar_tensor_tensor(pos[:], agg[:], 0.0, mid_t[b][:], ALU.max, ALU.add))
                dve.wait_ge(neg_exped, t + 1)
                dve.wait_ge(stored, value)
                return V.scalar_tensor_tensor(out_t[b][:], neg_exp[:], -1.0, pos[:], ALU.add, ALU.add)

            def scores(t, b, slots, step):
                dst = gath[b][:, 0:slots, FEAT:GROW].rearrange("p k h -> p h k")
                e = score[:, :, 0:slots]
                step(V.tensor_tensor(e, dst, column(src_score, t).unsqueeze(2).to_broadcast([ROWS, HEADS, slots]), ALU.add))
                step(V.scalar_tensor_tensor(e, e, SLOPE, e, ALU.mult, ALU.max))

            def weigh(b, slots, step, into):
                g = gath[b][:, 0:slots, 0:FEAT]
                w = prob[:, :, 0:slots].rearrange("p h k -> p k h").unsqueeze(3).to_broadcast([ROWS, slots, HEADS, HDIM])
                g_h = g.rearrange("p k (h d) -> p k h d", h=HEADS)
                step(V.tensor_tensor(g_h, g_h, w, ALU.mult))
                return V.tensor_reduce(into[:], g.rearrange("p k f -> p f k"), AX.X, ALU.add)

            with dve.If(bad_rows == 0):
                dve.sem_inc(attn_buffers_free, 2)
                for b in range(2):
                    dve.reg_mov(expected[b], 0)

                def stage_list(q):
                    dve.wait_ge(scattered[q.b], ALL * (TILES // 2 + q.half))
                    V.tensor_copy(stage[q.s][:], column(records, q.number)).then_inc(stage_ready, 1)

                def attend(q):
                    t, b = q.number, q.b
                    dve.wait_ge(stage_ready, t + 1)
                    dve.sem_inc(dve_holds, 1)
                    length = longest(dve, q.s)

                    def with_slots(slots):
                        step = stepper(dve, attn_step)
                        landed(b, attn_gathered[b], slots)
                        e = score[:, :, 0:slots]
                        scores(t, b, slots, step)
                        step(V.tensor_reduce(peak[:], e, AX.X, ALU.max))
                        V.tensor_tensor(e, e, peak[:].unsqueeze(2).to_broadcast([ROWS, HEADS, slots]), ALU.subtract).then_inc(score_made, 1)
                        dve.wait_ge(prob_made, t + 1)
                        V.tensor_reduce(total[:], prob[:, :, 0:slots], AX.X, ALU.add)
                        weigh(b, slots, step, agg).then_inc(agg_made, 1)
                    by_level(dve, length, LEVELS, with_slots)
                    dve.wait_ge(agg_made, t + 1)
                    dve.sem_inc(attn_buffers_free, 1)
                    step = stepper(dve, attn_step)
                    dve.wait_ge(mid_loaded[b], ALL * (q.half + 1))
                    finish(t, b, step, scattered[b], ALL * (1 + TILES // 2 + q.half)).then_inc(out_ready, 1)
                    dve.wait_ge(out_ready, t + 1)
                    dve.sem_inc(out_made, 1)

                for b in range(2):
                    dve.wait_ge(scattered[b], ALL * (1 + TILES // 2))
                for j in range(2):
                    stage_list(Tile(0, j))

                def attn_turn(q):
                    if not (isinstance(q.v, int) and q.number + 2 >= TILES):
                        stage_list(q.plus(2))
                    attend(q)
                sorted_tiles(dve, attn_turn)
            with dve.Else():
                mask = adj_in[0][:].bitcast(f32)
                dve.sem_inc(dense_free, 2)
                dve.sem_inc(dense_mask_free, 1)
                dve.sem_inc(dense_out_stored, ALL)
                with dve.Fori(0, TILES) as t:
                    step = stepper(dve, dense_step)
                    dve.wait_ge(dense_adj_loaded, ALL * (t + 1))
                    step(V.tensor_scalar(mask, adj_in[0][:], 0.0, None, ALU.not_equal))
                    step(V.memset(nb_max[:], 0.0))
                    with dve.Fori(0, BLOCKS // 2) as c2:
                        for b in range(2):
                            step = stepper(dve, dense_step)
                            dve.wait_ge(dense_loaded[b], ALL * (t * (BLOCKS // 2) + c2 + 1))
                            g = gath[b][:, :, 0:FEAT]
                            m = mask[:, bass.ds((2 * c2 + b) * BLOCK, BLOCK)].unsqueeze(2).to_broadcast([ROWS, BLOCK, FEAT])
                            step(V.tensor_tensor(g, g, m, ALU.mult))
                            step(V.tensor_reduce(part[:], g.rearrange("p k f -> p f k"), AX.X, ALU.max))
                            step(V.tensor_tensor(nb_max[:], nb_max[:], part[:], ALU.max))
                            dve.sem_inc(dense_free, 1)
                    step = stepper(dve, post_step)
                    dve.wait_ge(dense_x_loaded, ALL * (t + 1))
                    post(t + TILES, 0, ALL * (1 + TILES // 2 + t), step)
                    dve.sem_inc(dense_mask_free, 1)

                agg_h = agg[:].rearrange("p (h d) -> p h d", h=HEADS)
                with dve.Fori(0, TILES) as t:
                    step = stepper(dve, dense_step)
                    dve.wait_ge(dense_adj_loaded, ALL * (t + 1 + TILES))
                    step(V.tensor_scalar(mask, adj_in[0][:], 0.0, None, ALU.is_gt))
                    step(V.memset(peak_new[:], -3.0e38))
                    step(V.memset(total[:], 0.0))
                    step(V.memset(agg[:], 0.0))
                    with dve.Fori(0, BLOCKS // 2) as c2:
                        for b in range(2):
                            step = stepper(dve, dense_step)
                            n = t * BLOCKS + 2 * c2 + b
                            dve.wait_ge(dense_loaded[b], ALL * (t * (BLOCKS // 2) + c2 + 1 + TILES * (BLOCKS // 2)))
                            m1 = mask[:, bass.ds((2 * c2 + b) * BLOCK, BLOCK)]
                            scores(t, b, BLOCK, step)
                            step(V.tensor_tensor(score[:], score[:], m1.unsqueeze(1).to_broadcast([ROWS, HEADS, BLOCK]), ALU.mult))
                            step(V.tensor_scalar(is_nb[:], m1, -1.0, MASKED, ALU.add, ALU.mult))
                            step(V.tensor_tensor(score[:], score[:], is_nb[:].unsqueeze(1).to_broadcast([ROWS, HEADS, BLOCK]), ALU.add))
                            step(V.tensor_copy(peak[:], peak_new[:]))
                            step(V.tensor_reduce(part_sum[:], score[:], AX.X, ALU.max))
                            step(V.tensor_tensor(peak_new[:], peak[:], part_sum[:], ALU.max))
                            step(V.tensor_tensor(peak[:], peak[:], peak_new[:], ALU.subtract))
                            V.tensor_tensor(score[:], score[:], peak_new[:].unsqueeze(2).to_broadcast([ROWS, HEADS, BLOCK]),
                                            ALU.subtract).then_inc(dense_score, 1)
                            dve.wait_ge(dense_exp, n + 1)
                            step(V.tensor_reduce(part_sum[:], prob[:], AX.X, ALU.add))
                            step(V.tensor_tensor(total[:], total[:], rescale[:], ALU.mult))
                            step(weigh(b, BLOCK, step, part))
                            step(V.tensor_tensor(total[:], total[:], part_sum[:], ALU.add))
                            step(V.tensor_tensor(agg_h, agg_h, rescale[:].unsqueeze(2).to_broadcast([ROWS, HEADS, HDIM]), ALU.mult))
                            step(V.tensor_tensor(agg[:], agg[:], part[:], ALU.add))
                            dve.sem_inc(dense_free, 1)
                    dve.wait_ge(mid_loaded[0], ALL * (t + 1))
                    finish(t, 0, step, dense_out_stored, ALL * (t + 1)).then_inc(out_made, 1)
                    dve.wait_ge(out_made, t + 1)
                    dve.sem_inc(dense_mask_free, 1)


def kernel(x, adj, L1_gnn_W, L1_gnn_a):
    import numpy as np
    import concourse.bacc as bacc
    from concourse.bass_utils import run_bass_kernel_spmd

    arrays = {"x": np.asarray(x), "adj": np.asarray(adj), "weight": np.asarray(L1_gnn_W), "attn": np.asarray(L1_gnn_a)}
    nc = bacc.Bacc("TRN2", target_bir_lowering=False, num_devices=1)
    args = [nc.dram_tensor(n, a.shape, mybir.dt.from_np(a.dtype), kind="ExternalInput").ap() for n, a in arrays.items()]
    out = nc.dram_tensor("out", (NODES, FEAT), mybir.dt.float32, kind="ExternalOutput").ap()
    gnn_program(nc, *args, out)
    return run_bass_kernel_spmd(nc, [arrays], core_ids=[0]).results[0]["out"]
```

```python
from contextlib import ExitStack

import concourse.bass as bass
import concourse.mybir as mybir

NODES = 8192
FEAT = 128
HEADS = 4
HDIM = FEAT // HEADS
ROWS = 128
TILES = NODES // ROWS
CHUNK = 128
CHUNKS = NODES // CHUNK
SLOTS = 64
HALVES = [slice(0, NODES // 2), slice(NODES // 2, NODES)]
PICKS = 2 * (SLOTS // 8) - 1
GROW = FEAT + HEADS
WINDOW = 8
PLACES = WINDOW * ROWS
LEAD = WINDOW + 2
BLOCK_ORDER = [4, 1, 5, 0, 6, 2, 3, 7]
COUNT, NODE, NODE1 = SLOTS, SLOTS + 1, SLOTS + 2
RECORD = SLOTS + 3
LEVELS = [*range(26, 42), 44, 47, *range(50, 57), 60, 64]
DIGIT = 128
BLOCK = SLOTS
BLOCKS = NODES // BLOCK
EPS = 1e-5
SLOPE = 0.2
MASKED = 9.0e15
PAD_SCORE = -1.0e17
ALL = 16


def gnn_program(nc, x, adj, weight, attn, out):
    f32, bf16, i32, u32 = mybir.dt.float32, mybir.dt.bfloat16, mybir.dt.int32, mybir.dt.uint32
    ALU, ACT, AX = mybir.AluOpType, mybir.ActivationFunctionType, mybir.AxisListType

    node_table = nc.dram_tensor("node_table", (NODES + 1, FEAT), f32).ap()
    attn_table = nc.dram_tensor("attn_table", (NODES + 1, GROW), f32).ap()
    x_sorted = nc.dram_tensor("x_sorted", (NODES, FEAT), f32).ap()
    mid = nc.dram_tensor("mid", (NODES, FEAT), f32).ap()

    ctx = ExitStack()
    with ctx:
        def sb(name, shape, dt=f32):
            return ctx.enter_context(nc.sbuf_tensor(name, shape, dt))

        def ps(name, shape):
            return ctx.enter_context(nc.psum_tensor(name, shape, f32))

        def sem(name):
            return ctx.enter_context(nc.semaphore(name))

        adj_in = [sb(f"adj_in{b}", [ROWS, NODES], i32) for b in range(2)]
        keys = sb("keys", [ROWS, NODES], bf16)
        gath = [sb(f"gath{b}", [ROWS, SLOTS, GROW]) for b in range(2)]
        records = sb("records", [ROWS, TILES, RECORD], mybir.dt.int16)
        stage = [sb(f"stage{s}", [ROWS, RECORD], u32) for s in range(4)]
        built = sb("built", [ROWS, WINDOW, RECORD])
        node_number = sb("node_number", [ROWS, TILES, 2])
        tie = sb("tie", [ROWS, WINDOW])
        sort_key = sb("sort_key", [ROWS, WINDOW])
        int_space = [sb(f"int_space{d}", [ROWS, max(CHUNKS * 8, WINDOW * RECORD)], u32) for d in range(2)]
        built_int, digit_int = (v[:, 0:WINDOW * RECORD].rearrange("p (k r) -> p k r", r=RECORD) for v in int_space)
        cands = [v[:, 0:CHUNKS * 8].bitcast(f32).rearrange("p (c k) -> p c k", k=8) for v in int_space]
        digits = [sb(f"digits{d}", [ROWS, WINDOW, RECORD], bf16) for d in range(2)]
        standing = sb("standing", [ROWS, WINDOW])
        place_number = sb("place_number", [ROWS, PLACES], mybir.dt.int16)
        onehot = sb("onehot", [ROWS, WINDOW, PLACES], bf16)
        key_diag = onehot[:, 0:2, :].rearrange("p k n -> p (k n)").bitcast(f32).rearrange("p (k r) -> p k r", r=ROWS)
        column_number = sb("column_number", [ROWS, CHUNK], bf16)
        chunk_base = sb("chunk_base", [ROWS, CHUNKS])
        is_nb = sb("is_nb", [ROWS, SLOTS])
        square_sum = sb("square_sum", [ROWS, TILES])
        listed = sb("listed", [ROWS, TILES])
        x_window = sb("x_window", [ROWS, WINDOW, FEAT])
        x_t = [sb(f"x_t{b}", [ROWS, FEAT]) for b in range(2)]
        mid_t = [sb(f"mid_t{b}", [ROWS, FEAT]) for b in range(2)]
        row_t = [sb(f"row_t{b}", [ROWS, GROW]) for b in range(2)]
        src_score = sb("src_score", [ROWS, TILES, HEADS])
        nb_max = sb("nb_max", [ROWS, FEAT])
        bn = sb("bn", [ROWS, 6])
        mean_var = sb("mean_var", [ROWS, 2])
        std = sb("std", [ROWS, 1])
        rstd = sb("rstd", [ROWS, 1])
        shift = sb("shift", [ROWS, 1])
        normed = sb("normed", [ROWS, FEAT])
        normed_T = sb("normed_T", [FEAT, ROWS])
        sums, neg_mean, var_sums, shifts = (sb(name, [ROWS, TILES]) for name in ("sums", "neg_mean", "var_sums", "shifts"))
        stat_r = sb("stat_r", [ROWS, TILES])
        eps_t = sb("eps_t", [ROWS, 1])
        quarter = sb("quarter", [ROWS, 1])
        ones = sb("ones", [ROWS, ROWS])
        ident = sb("ident", [ROWS, ROWS])
        w_cat = sb("w_cat", [FEAT, FEAT + 2 * HEADS])
        w_T = sb("w_T", [FEAT, FEAT])
        a_blocks = sb("a_blocks", [FEAT, 2 * HEADS])
        pad_row = sb("pad_row", [1, GROW])
        space = sb("space", [ROWS, max(CHUNKS * 8, 2 * HEADS * SLOTS)])
        cand_base = space[:, 0:CHUNKS * 8].rearrange("p (c k) -> p c k", k=8)
        score, prob = (space[:, d * HEADS * SLOTS:(d + 1) * HEADS * SLOTS].rearrange("p (h k) -> p h k", h=HEADS) for d in range(2))
        peak = sb("peak", [ROWS, HEADS])
        total = sb("total", [ROWS, HEADS])
        x_rest = sb("x_rest", [ROWS, WINDOW, FEAT])
        x_last = sb("x_last", [ROWS, WINDOW, FEAT], bf16)
        x_parts = [v[:].rearrange("p k f -> p (k f)").bitcast(bf16).rearrange("p (k f two) -> p k f two", k=WINDOW, two=2)[:, :, :, 1]
                   for v in (x_window, x_rest)] + [x_last[:]]
        agg, neg, neg_exp, pos = (x_last[:].rearrange("p k f -> p (k f)").bitcast(f32)[:, d * FEAT:(d + 1) * FEAT] for d in range(4))
        out_t = [sb(f"out_t{b}", [ROWS, FEAT]) for b in range(2)]
        bad = sb("bad", [ROWS, TILES])
        empty = sb("empty", [ROWS, TILES])
        bad_row = sb("bad_row", [ROWS, 1])
        bad_count = sb("bad_count", [1, 1], i32)
        peak_new = sb("peak_new", [ROWS, HEADS])
        rescale = sb("rescale", [ROWS, HEADS])
        part = pos
        part_sum = sb("part_sum", [ROWS, HEADS])

        p_keys = ps("p_keys", [ROWS, PLACES])
        p_x = p_keys[:].rearrange("p (k f) -> p k f", f=FEAT)
        p_sorted = ps("p_sorted", [ROWS, WINDOW, ROWS])
        p_T = ps("p_T", [FEAT, ROWS])
        p_row = ps("p_row", [ROWS, FEAT + 2 * HEADS])
        p_w = ps("p_w", [FEAT, FEAT])
        p_small = ps("p_small", [FEAT, 2 * HEADS + 1])
        p_a = p_small[:, 0:2 * HEADS]
        p_bad = p_small[0:1, 2 * HEADS:]

        weights_loaded = sem("weights_loaded")
        a_zeroed = sem("a_zeroed")
        a_loaded = sem("a_loaded")
        all_x_loaded = sem("all_x_loaded")
        const_made = sem("const_made")
        pad_made = sem("pad_made")
        setup = sem("setup")
        var_made = sem("var_made")
        std_made = sem("std_made")
        sums_made = sem("sums_made")
        neg_mean_made = sem("neg_mean_made")
        shifts_made = sem("shifts_made")
        nodes_relued = sem("nodes_relued")
        nodes_stored = sem("nodes_stored")
        wT_done = sem("wT_done")
        wT_copied = sem("wT_copied")
        wa_done = sem("wa_done")
        w_ready = sem("w_ready")
        first_half_loaded = sem("first_half_loaded")
        adj_loaded = [sem(f"adj_loaded{b}") for b in range(2)]
        cast_done = sem("cast_done")
        squares_done = sem("squares_done")
        keys_used = sem("keys_used")
        build_step = sem("build_step")
        diag_made = sem("diag_made")
        keys_spread = sem("keys_spread")
        onehots_made = sem("onehots_made")
        standing_made = sem("standing_made")
        digits_made = sem("digits_made")
        sorted_done = sem("sorted_done")
        records_made = sem("records_made")
        x_window_loaded = sem("x_window_loaded")
        x_split = sem("x_split")
        x_permuted = sem("x_permuted")
        x_taken = sem("x_taken")
        x_stored = sem("x_stored")
        x_loaded = [sem(f"x_loaded{b}") for b in range(2)]
        list_ready = sem("list_ready")
        dve_holds = sem("dve_holds")
        gathered = [sem(f"gathered{b}") for b in range(2)]
        buffers_free = sem("buffers_free")
        max_made = sem("max_made")
        pool_holds = sem("pool_holds")
        post_step = sem("post_step")
        tile_var = sem("tile_var")
        tile_std = sem("tile_std")
        shift_made = sem("shift_made")
        mid_made = sem("mid_made")
        tile_normed = sem("tile_normed")
        transposed = sem("transposed")
        T_copied = sem("T_copied")
        projected = sem("projected")
        row_made = sem("row_made")
        scattered = [sem(f"scattered{b}") for b in range(2)]
        mid_stored = [sem(f"mid_stored{b}") for b in range(2)]
        check_step = sem("check_step")
        bad_row_made = sem("bad_row_made")
        bad_summed = sem("bad_summed")
        verdict = sem("verdict")
        stage_ready = sem("stage_ready")
        attn_gathered = [sem(f"attn_gathered{b}") for b in range(2)]
        attn_buffers_free = sem("attn_buffers_free")
        agg_made = sem("agg_made")
        out_ready = sem("out_ready")
        attn_step = sem("attn_step")
        score_made = sem("score_made")
        prob_made = sem("prob_made")
        neg_made = sem("neg_made")
        neg_exped = sem("neg_exped")
        mid_loaded = [sem(f"mid_loaded{b}") for b in range(2)]
        out_made = sem("out_made")
        dense_out_stored = sem("dense_out_stored")
        dense_x_loaded = sem("dense_x_loaded")
        dense_row_stored = sem("dense_row_stored")
        dense_adj_loaded = sem("dense_adj_loaded")
        dense_mask_free = sem("dense_mask_free")
        dense_loaded = [sem(f"dense_loaded{b}") for b in range(2)]
        dense_free = sem("dense_free")
        dense_step = sem("dense_step")
        dense_score = sem("dense_score")
        dense_exp = sem("dense_exp")

        block = ctx.enter_context(nc.Block())

        adj_rows = adj.rearrange("(t p) n -> t p n", p=ROWS)
        x_rows = x.rearrange("(t p) f -> t p f", p=ROWS)
        x_windows = x.rearrange("(w k p) f -> w p k f", k=WINDOW, p=ROWS)
        x_sorted_windows = x_sorted.rearrange("(w k p) f -> w p k f", k=WINDOW, p=ROWS)
        x_sorted_rows = x_sorted.rearrange("(t p) f -> t p f", p=ROWS)
        mid_rows = mid.rearrange("(t p) f -> t p f", p=ROWS)
        out_rows = out.rearrange("(t p) f -> t p f", p=ROWS)
        attn_rows = attn_table[1:NODES + 1, :].rearrange("(t p) f -> t p f", p=ROWS)
        node_blocks = node_table[1:NODES + 1, :].rearrange("(c k) f -> c k f", k=BLOCK)
        attn_blocks = attn_table[1:NODES + 1, :].rearrange("(c k) f -> c k f", k=BLOCK)
        all_x = gath[0][:, 0:TILES, 0:FEAT]
        all_sq = gath[1][:, 0:TILES, 0:FEAT]

        class Tile:

            def __init__(self, v, j):
                self.v, self.j = v, j
                self.number = WINDOW * v + j
                self.half = (WINDOW // 2) * v + j // 2
                self.b, self.s, self.k = j % 2, j % 4, j % WINDOW
                self.window = v + j // WINDOW

            def plus(self, d):
                return Tile(self.v, self.j + d)

        def tile_of(rows, t):
            return rows[bass.ds(t, 1), :, :].rearrange("o p f -> (o p) f")

        def window_of(windows, w):
            return windows[bass.ds(w, 1), :, :, :].rearrange("o p k f -> (o p) k f")

        def column(tensor, t):
            return tensor[:, bass.ds(t, 1), :].rearrange("p o c -> p (o c)")

        class Chain:

            def __init__(self, engine, semaphore):
                self.engine, self.semaphore, self.count = engine, semaphore, 0
                engine.sem_clear(semaphore)

            def did(self, ins):
                self.count += 1
                ins.then_inc(self.semaphore, 1)

            def wait(self):
                self.engine.wait_ge(self.semaphore, self.count)

            def __call__(self, ins):
                self.did(ins)
                self.wait()

        def steps(engine, body):
            for j in range(LEAD):
                body(Tile(0, j), None)
            turns = (TILES - 2 * WINDOW) // WINDOW
            with engine.Fori(0, turns) as v:
                for j in range(WINDOW):
                    body(Tile(v, j + LEAD), Tile(v, j))
            for j in range(turns * WINDOW, TILES):
                body(Tile(0, j + LEAD) if j + LEAD < TILES else None, Tile(0, j))

        def window_due(n, q, turns):
            now = q.plus(LEAD) if n is None else n
            if now.k != turns - 1 or (isinstance(now.v, int) and not WINDOW <= now.number < TILES + WINDOW):
                return None
            return now.window - 1

        def sorted_tiles(engine, body):
            with engine.Fori(0, TILES // WINDOW - 1) as v:
                for j in range(WINDOW):
                    body(Tile(v, j))
            for j in range(TILES - WINDOW, TILES):
                body(Tile(0, j))

        def level_of(slot):
            return max([level for level in LEVELS if level <= slot], default=0)

        def by_level(engine, length, levels, body):
            if len(levels) == 1:
                body(levels[0])
                return
            mid_level = len(levels) // 2
            with engine.If(length <= levels[mid_level - 1]):
                by_level(engine, length, levels[:mid_level], body)
            with engine.Else():
                by_level(engine, length, levels[mid_level:], body)

        def longest(engine, s):
            return engine.value_load(stage[s][0:1, COUNT:COUNT + 1], min_val=0, max_val=SLOTS)

        @block.sync
        def _(sp):
            sp.sem_inc(squares_done, 2)

            def load_adj(n):
                sp.wait_ge(squares_done, n.number + 1)
                sp.dma_start(adj_in[n.b][:], tile_of(adj_rows, n.number)).then_inc(adj_loaded[n.b], ALL)

            for half, loaded in zip(HALVES, (first_half_loaded, adj_loaded[0])):
                sp.dma_start(adj_in[0][:, half], tile_of(adj_rows, 0)[:, half]).then_inc(loaded, ALL)
            load_adj(Tile(0, 1))
            sp.dma_start(all_x, x.rearrange("(t p) f -> p t f", p=ROWS)).then_inc(all_x_loaded, ALL)
            sp.dma_start(x_window[:], window_of(x_windows, 0)).then_inc(x_window_loaded, ALL)
            sp.dma_start(w_cat[:, 0:FEAT], weight).then_inc(weights_loaded, ALL)
            sp.wait_ge(a_zeroed, 1)
            for h in range(HEADS):
                for col, lo in ((h, HDIM), (HEADS + h, 0)):
                    sp.dma_start(a_blocks[h * HDIM:(h + 1) * HDIM, col:col + 1],
                                 attn[0, h, lo:lo + HDIM].unsqueeze(1)).then_inc(a_loaded, ALL)

            def turn(n, q):
                if n is not None and not (isinstance(n.v, int) and n.number + 2 >= TILES):
                    load_adj(n.plus(2))
                if q is None and n.number == WINDOW - 1:
                    sp.wait_ge(nodes_relued, TILES // 4)
                    sp.dma_start(node_table[1:NODES + 1, :].rearrange("(t p) f -> p t f", p=ROWS), all_x).then_inc(nodes_stored, ALL)
                w = window_due(n, q, 2)
                if w is not None:
                    sp.wait_ge(x_taken, w + 2)
                    sp.dma_start(window_of(x_sorted_windows, w), x_window[:]).then_inc(x_stored, ALL)
                    if n is not None:
                        sp.wait_ge(x_stored, ALL * (w + 1))
                        sp.dma_start(x_window[:], window_of(x_windows, w + 1)).then_inc(x_window_loaded, ALL)
                if q is not None:
                    sp.wait_ge(mid_made, q.number + 1)
                    sp.dma_start(tile_of(mid_rows, q.number), mid_t[q.b][:]).then_inc(mid_stored[q.b], ALL)
                after = q.plus(1) if q is not None else n.plus(1 - LEAD)
                if q is None and n.number + 1 < LEAD or q is not None and isinstance(q.v, int) and q.number + 1 == TILES:
                    return
                sp.wait_ge(x_stored, ALL * (after.window + 1))
                sp.dma_start(x_t[after.b][:], tile_of(x_sorted_rows, after.number)).then_inc(x_loaded[after.b], ALL)
            steps(sp, turn)

            for b in range(2):
                sp.wait_ge(mid_stored[b], ALL * (1 + TILES // 2))
            sp.wait_ge(verdict, 1)
            bad_rows = sp.value_load(bad_count[0:1, 0:1], min_val=0, max_val=ROWS)
            with sp.If(bad_rows == 0):
                sp.sem_inc(out_made, 2)

                def load_mid(q):
                    sp.wait_ge(out_made, q.number + 1)
                    sp.dma_start(mid_t[q.b][:], tile_of(mid_rows, q.number)).then_inc(mid_loaded[q.b], ALL)
                sorted_tiles(sp, load_mid)
            with sp.Else():
                def dense_blocks(t_all, rows_of, width):
                    with sp.Fori(0, BLOCKS // 2) as c2:
                        for b in range(2):
                            n = t_all * BLOCKS + 2 * c2 + b
                            sp.wait_ge(dense_free, n + 1)
                            src = rows_of[bass.ds(2 * c2 + b, 1), :, :].rearrange("o k f -> (o k) f")
                            sp.dma_start(gath[b][:, :, 0:width], src.unsqueeze(0).to_broadcast([ROWS, BLOCK, width])).then_inc(dense_loaded[b], ALL)

                for b in range(2):
                    sp.wait_ge(scattered[b], ALL * (1 + TILES // 2))
                with sp.Fori(0, TILES) as t:
                    sp.wait_ge(dense_mask_free, t + 1)
                    sp.dma_start(adj_in[0][:], tile_of(adj_rows, t)).then_inc(dense_adj_loaded, ALL)
                    sp.dma_start(x_t[0][:], tile_of(x_rows, t)).then_inc(dense_x_loaded, ALL)
                    dense_blocks(t, node_blocks, FEAT)
                    sp.wait_ge(mid_made, t + TILES + 1)
                    sp.dma_start(tile_of(mid_rows, t), mid_t[0][:]).then_inc(mid_stored[0], ALL)
                    sp.wait_ge(row_made, t + TILES + 1)
                    sp.dma_start(tile_of(attn_rows, t), row_t[0][:]).then_inc(dense_row_stored, ALL)
                sp.wait_ge(mid_stored[0], ALL * (1 + TILES // 2 + TILES))
                sp.wait_ge(dense_row_stored, ALL * (1 + TILES))
                with sp.Fori(0, TILES) as t:
                    sp.wait_ge(dense_mask_free, t + TILES + 1)
                    sp.dma_start(adj_in[0][:], tile_of(adj_rows, t)).then_inc(dense_adj_loaded, ALL)
                    sp.dma_start(mid_t[0][:], tile_of(mid_rows, t)).then_inc(mid_loaded[0], ALL)
                    dense_blocks(t + TILES, attn_blocks, GROW)
                    sp.wait_ge(out_made, t + 1)
                    sp.dma_start(tile_of(out_rows, t), out_t[0][:]).then_inc(dense_out_stored, ALL)
                sp.wait_ge(dense_out_stored, ALL * (1 + TILES))

        @block.gpsimd
        def _(pool):
            pool.memset(a_blocks[:], 0.0).then_inc(a_zeroed, 1)

            def numbers(tensor, pattern, base, step):
                pool.iota(tensor, pattern=pattern, base=base, channel_multiplier=step,
                          allow_small_or_imprecise_dtypes=True).then_inc(const_made, 1)
            numbers(column_number[:], [[1, CHUNK]], 1, 0)
            numbers(chunk_base[:], [[CHUNK, CHUNKS]], 0, 0)
            numbers(node_number[:], [[ROWS, TILES], [1, 2]], 0, 1)
            numbers(place_number[:], [[-2, PLACES]], PLACES - 1, 0)
            numbers(tie[:], [[ROWS, WINDOW]], 0, 1)
            pool.memset(ident[:], 0.0).then_inc(const_made, 1)
            pool.wait_ge(const_made, 6)
            pool.affine_select(out=ident[:], in_=ident[:], compare_op=ALU.not_equal, fill=1.0, base=0,
                               pattern=[[-1, ROWS]], channel_multiplier=1).then_inc(const_made, 1)
            pool.memset(eps_t[:], EPS).then_inc(const_made, 1)
            pool.memset(quarter[:], -0.25).then_inc(const_made, 1)
            pool.memset(ones[:], 1.0).then_inc(const_made, 1)
            pool.memset(pad_row[:, 0:FEAT], 0.0).then_inc(pad_made, 1)
            pool.memset(pad_row[:, FEAT:GROW], PAD_SCORE).then_inc(pad_made, 1)
            pool.wait_ge(pad_made, 2)
            pool.dma_start(node_table[0:1, :], pad_row[:, 0:FEAT]).then_inc(scattered[0], ALL)
            pool.dma_start(attn_table[0:1, :], pad_row[:, :]).then_inc(scattered[1], ALL)
            pool.wait_ge(nodes_stored, ALL)
            for b in range(2):
                pool.wait_ge(scattered[b], ALL)

            def gather_row(dst, table, s, col, done):
                pool.indirect_dma_start(dst, None, table, bass.IndirectOffsetOnAxis(ap=stage[s][:, col:col + 1], axis=0)).then_inc(done, ALL)

            def gather(table, width, q, done):
                def slots_from(first):
                    if first == SLOTS:
                        return
                    with pool.If(length > level_of(first)):
                        end = min(first + 8, SLOTS)
                        for k in range(first, end):
                            if level_of(k) == level_of(first):
                                gather_row(gath[q.b][:, k, 0:width], table, q.s, k, done)
                                continue
                            with pool.If(length > level_of(k)):
                                gather_row(gath[q.b][:, k, 0:width], table, q.s, k, done)
                            with pool.Else():
                                pool.nop()
                        slots_from(end)
                    with pool.Else():
                        pool.nop()
                for k in range(LEVELS[0]):
                    gather_row(gath[q.b][:, k, 0:width], table, q.s, k, done)
                length = longest(pool, q.s)
                slots_from(LEVELS[0])

            def gather_max(q):
                pool.wait_ge(buffers_free, q.number + 1)
                pool.sem_inc(pool_holds, 1)
                pool.wait_ge(list_ready, q.number + 1)
                pool.sem_inc(pool_holds, 1)
                gather(node_table, FEAT, q, gathered[q.b])

            def scatter_row(q):
                pool.wait_ge(row_made, q.number + 1)
                pool.sem_inc(pool_holds, 1)
                pool.indirect_dma_start(attn_table, bass.IndirectOffsetOnAxis(ap=stage[q.s][:, NODE1:NODE1 + 1], axis=0),
                                        row_t[q.b][:], None).then_inc(scattered[q.b], ALL)

            def turn(q):
                if not (isinstance(q.v, int) and q.number + 2 >= TILES):
                    gather_max(q.plus(2))
                scatter_row(q)
            for j in range(2):
                gather_max(Tile(0, j))
            sorted_tiles(pool, turn)

            pool.wait_ge(verdict, 1)
            bad_rows = pool.value_load(bad_count[0:1, 0:1], min_val=0, max_val=ROWS)
            with pool.If(bad_rows == 0):
                for b in range(2):
                    pool.wait_ge(scattered[b], ALL * (1 + TILES // 2))

                def gather_attn(q):
                    pool.wait_ge(attn_buffers_free, q.number + 1)
                    pool.sem_inc(pool_holds, 1)
                    pool.wait_ge(stage_ready, q.number + 1)
                    pool.sem_inc(pool_holds, 1)
                    gather(attn_table, GROW, q, attn_gathered[q.b])

                def scatter_out(q):
                    pool.wait_ge(out_ready, q.number + 1)
                    pool.sem_inc(pool_holds, 1)
                    pool.indirect_dma_start(out, bass.IndirectOffsetOnAxis(ap=stage[q.s][:, NODE:NODE + 1], axis=0),
                                            out_t[q.b][:], None).then_inc(scattered[q.b], ALL)

                def attn_turn(q):
                    if not (isinstance(q.v, int) and q.number == TILES - 1):
                        gather_attn(q.plus(1))
                    scatter_out(q)
                gather_attn(Tile(0, 0))
                sorted_tiles(pool, attn_turn)
                for b in range(2):
                    pool.wait_ge(scattered[b], ALL * (1 + TILES))
            with pool.Else():
                pool.nop()

        @block.tensor
        def _(pe):
            pe.wait_ge(const_made, 10)
            pe.wait_ge(weights_loaded, ALL)
            nc.tensor.transpose(p_w[:], w_cat[:, 0:FEAT], ident[:]).then_inc(wT_done, 1)
            pe.wait_ge(wT_copied, 1)
            pe.wait_ge(a_loaded, ALL * 2 * HEADS)
            nc.tensor.matmul(p_a, w_T[:], a_blocks[:], start=True, stop=True).then_inc(wa_done, 1)
            pe.wait_ge(w_ready, 1)

            def spread_keys(w):
                pe.wait_ge(diag_made, w + 1)
                pe.wait_ge(x_taken, w + 1)
                diag = key_diag.rearrange("p k r -> p (k r)")
                for c in range(0, PLACES, 512):
                    last = nc.tensor.matmul(p_keys[:, c:c + 512], ones[:], diag[:, c:c + 512], start=True, stop=True)
                last.then_inc(keys_spread, 1)

            def sort_window(w):
                pe.wait_ge(records_made, w + 1)
                pe.wait_ge(digits_made, w + 1)
                pe.wait_ge(onehots_made, w + 1)
                terms = [(k, d) for k in range(WINDOW) for d in range(2)]
                for q, place in enumerate(BLOCK_ORDER):
                    for k, d in terms:
                        last = nc.tensor.matmul(p_sorted[:, q, 0:RECORD], onehot[:, k, place * ROWS:(place + 1) * ROWS],
                                                digits[d][:, k, :], start=(k, d) == terms[0], stop=(k, d) == terms[-1])
                last.then_inc(sorted_done, 1)

            def permute_x(w):
                pe.wait_ge(x_split, w + 1)
                terms = [(k, d) for d in range(3) for k in range(WINDOW)]
                for q, place in enumerate(BLOCK_ORDER):
                    for k, d in terms:
                        last = nc.tensor.matmul(p_x[:, q, :], onehot[:, k, place * ROWS:(place + 1) * ROWS],
                                                x_parts[d][:, k, :], start=(k, d) == terms[0], stop=(k, d) == terms[-1])
                last.then_inc(x_permuted, 1)

            def project(s):
                pe.wait_ge(tile_normed, s + 1)
                nc.tensor.transpose(p_T[:], normed[:], ident[:]).then_inc(transposed, 1)
                pe.wait_ge(T_copied, s + 1)
                nc.tensor.matmul(p_row[:], normed_T[:], w_cat[:], start=True, stop=True).then_inc(projected, 1)

            def turn(n, q):
                window_built = n is not None and n.k == WINDOW - 1
                if window_built:
                    spread_keys(n.window)
                if q is not None:
                    project(q.number)
                if window_built:
                    sort_window(n.window)
                w = window_due(n, q, 1)
                if w is not None:
                    permute_x(w)
            steps(pe, turn)
            pe.wait_ge(bad_row_made, 1)
            nc.tensor.matmul(p_bad, bad_row[:], ones[:, 0:1], start=True, stop=True).then_inc(bad_summed, 1)
            pe.wait_ge(verdict, 1)
            bad_rows = pe.value_load(bad_count[0:1, 0:1], min_val=0, max_val=ROWS)
            with pe.If(bad_rows == 0):
                pe.nop()
            with pe.Else():
                with pe.Fori(0, TILES) as t:
                    project(t + TILES)

        @block.scalar
        def _(act):
            act.sem_inc(keys_used, 2)
            act.sem_inc(records_made, 1)
            act.sem_inc(x_taken, 1)
            act.wait_ge(const_made, 10)

            def over_tiles(h, body, done):
                with act.Fori(h * TILES // 8, (h + 1) * TILES // 8) as v:
                    for j in range(4):
                        last = body(4 * v + j)
                    last.then_inc(done, 1)

            def input_sums(h):
                act.wait_ge(all_x_loaded, ALL)
                over_tiles(h, lambda t: nc.scalar.activation(column(all_sq, t), column(all_x, t), ACT.Copy,
                                                             accum_out=sums[:, bass.ds(t, 1)]), sums_made)

            def input_variances(h):
                act.wait_ge(neg_mean_made, h + 1)
                over_tiles(h, lambda t: nc.scalar.activation(column(all_sq, t), column(all_x, t), ACT.Square, bias=neg_mean[:, bass.ds(t, 1)],
                                                             accum_out=var_sums[:, bass.ds(t, 1)]), var_made)

            def input_std():
                act.wait_ge(var_made, TILES // 4)
                nc.scalar.activation(stat_r[:], var_sums[:], ACT.Sqrt, bias=eps_t[:], scale=1.0 / FEAT).then_inc(std_made, 1)

            def input_normed(h):
                act.wait_ge(shifts_made, 1)
                over_tiles(h, lambda t: nc.scalar.activation(column(all_x, t), column(all_x, t), ACT.Relu, bias=shifts[:, bass.ds(t, 1)],
                                                             scale=stat_r[:, bass.ds(t, 1)]), nodes_relued)

            def cast(n):
                for d, half in enumerate(HALVES):
                    if d == 0 and isinstance(n.v, int) and n.number == 0:
                        act.wait_ge(first_half_loaded, ALL)
                    else:
                        act.wait_ge(adj_loaded[n.b], ALL * (n.half + 1))
                    act.wait_ge(keys_used, 2 * n.number + d + 1)
                    nc.scalar.activation(keys[:, half], adj_in[n.b][:, half], ACT.Copy).then_inc(cast_done, 1)

            def square(n):
                act.wait_ge(cast_done, 2 * n.number + 2)
                nc.scalar.activation(adj_in[n.b][:].bitcast(f32), adj_in[n.b][:], ACT.Square, bias=quarter[:],
                                     accum_out=square_sum[:, bass.ds(n.number, 1)]).then_inc(squares_done, 1)

            def compare_keys(w):
                act.wait_ge(keys_spread, w + 1)
                for k in range(WINDOW):
                    last = nc.scalar.activation(onehot[:, k, :], p_keys[:], ACT.Sign, scale=-1.0, bias=sort_key[:, k:k + 1],
                                                accum_out=standing[:, k:k + 1])
                last.then_inc(standing_made, 1)

            def take_records(w):
                act.wait_ge(sorted_done, w + 2)
                nc.scalar.activation(records[:, bass.ds(w * WINDOW, WINDOW), :], p_sorted[:, :, 0:RECORD],
                                     ACT.Copy).then_inc(records_made, 1)

            def take_x(w):
                act.wait_ge(x_permuted, w + 2)
                nc.scalar.activation(x_window[:], p_x, ACT.Copy).then_inc(x_taken, 1)

            def norm_and_row(t, s, b, stored, value):
                act.wait_ge(tile_var, s + 1)
                nc.scalar.activation(std[:], mean_var[:, 1:2], ACT.Sqrt, bias=eps_t[:]).then_inc(tile_std, 1)
                act.wait_ge(shift_made, s + 1)
                nc.scalar.activation(normed[:], mid_t[b][:], ACT.Relu, bias=shift[:], scale=rstd[:]).then_inc(tile_normed, 1)
                act.wait_ge(transposed, s + 1)
                nc.scalar.activation(normed_T[:], p_T[:], ACT.Copy).then_inc(T_copied, 1)
                act.wait_ge(projected, s + 1)
                act.wait_ge(stored, value)
                nc.scalar.activation(row_t[b][:], p_row[:, 0:GROW], ACT.Copy)
                nc.scalar.activation(column(src_score, t), p_row[:, GROW:], ACT.Copy).then_inc(row_made, 1)

            def join_weights():
                act.wait_ge(wT_done, 1)
                nc.scalar.activation(w_T[:], p_w[:], ACT.Copy).then_inc(wT_copied, 1)
                act.wait_ge(wa_done, 1)
                act.wait_ge(weights_loaded, ALL)
                nc.scalar.activation(w_cat[:, FEAT:], p_a, ACT.Copy).then_inc(w_ready, 1)

            cast(Tile(0, 0))
            square(Tile(0, 0))

            def meanwhile(n):
                if n in (0, 1):
                    input_sums(n)
                if n in (2, 3):
                    input_variances(n - 2)
                if n == 3:
                    input_std()
                if n == 4:
                    join_weights()
                if n in (5, 6):
                    input_normed(n - 5)

            def turn(n, q):
                more = n is not None and not (isinstance(n.v, int) and n.number + 1 >= TILES)
                if more:
                    cast(n.plus(1))
                if q is None:
                    meanwhile(n.number)
                if q is not None:
                    norm_and_row(q.number, q.number, q.b, scattered[q.b], ALL * (q.half + 1))
                if n is not None and n.k == WINDOW - 1:
                    compare_keys(n.window)
                if more:
                    square(n.plus(1))
                if n is not None and n.k == WINDOW - 1:
                    take_records(n.window)
                w = window_due(n, q, 1)
                if w is not None:
                    take_x(w)
            steps(act, turn)

            act.wait_ge(verdict, 1)
            bad_rows = act.value_load(bad_count[0:1, 0:1], min_val=0, max_val=ROWS)

            def elu_exp(t):
                act.wait_ge(neg_made, t + 1)
                nc.scalar.activation(neg_exp, neg, ACT.Exp).then_inc(neg_exped, 1)

            with act.If(bad_rows == 0):
                with act.Fori(0, TILES) as t:
                    act.wait_ge(score_made, t + 1)
                    nc.scalar.activation(prob, score, ACT.Exp).then_inc(prob_made, 1)
                    elu_exp(t)
            with act.Else():
                act.sem_inc(dense_row_stored, ALL)
                for b in range(2):
                    act.wait_ge(scattered[b], ALL * (1 + TILES // 2))
                with act.Fori(0, TILES) as t:
                    norm_and_row(t, t + TILES, 0, dense_row_stored, ALL * (t + 1))
                with act.Fori(0, TILES) as t:
                    with act.Fori(0, BLOCKS) as c:
                        act.wait_ge(dense_score, t * BLOCKS + c + 1)
                        nc.scalar.activation(prob, score, ACT.Exp)
                        nc.scalar.activation(rescale[:], peak[:], ACT.Exp).then_inc(dense_exp, 1)
                    elu_exp(t)

        @block.vector
        def _(dve):
            V = nc.vector
            dve.sem_inc(buffers_free, 2)
            dve.sem_inc(sorted_done, 1)
            dve.sem_inc(x_permuted, 1)
            for b in range(2):
                dve.sem_inc(mid_stored[b], ALL)
            dve.wait_ge(const_made, 10)

            def input_means(h):
                dve.wait_ge(sums_made, (h + 1) * TILES // 8)
                half = slice(h * TILES // 2, (h + 1) * TILES // 2)
                V.tensor_scalar(neg_mean[:, half], sums[:, half], -1.0 / FEAT, None, ALU.mult).then_inc(neg_mean_made, 1)

            def input_shifts():
                step = Chain(dve, setup)
                dve.wait_ge(std_made, 1)
                step(V.reciprocal(stat_r[:], stat_r[:]))
                V.tensor_tensor(shifts[:], neg_mean[:], stat_r[:], ALU.mult).then_inc(shifts_made, 1)

            def pick(n, i, step):
                flat = cands[n.b].rearrange("p c k -> p (c k)")
                eight = built[:, n.k, i // 2 * 8:i // 2 * 8 + 8]
                step.wait()
                step.did(V.match_replace(flat, eight, flat, 0.0) if i % 2 else V.max(eight, flat))

            def count(n):
                return V.tensor_scalar(is_nb[:], built[:, n.k, 0:SLOTS], 0.0, 0.0, ALU.is_gt, ALU.add,
                                       accum_out=built[:, n.k, COUNT:COUNT + 1])

            def read_length(q):
                dve.wait_ge(list_ready, q.number + 1)
                dve.sem_inc(dve_holds, 1)
                return longest(dve, q.s)

            def build(n, q):
                length = None
                step = Chain(dve, build_step)
                cand = cands[n.b]
                for d, half in enumerate(HALVES):
                    dve.wait_ge(cast_done, 2 * n.number + d + 1)
                    by_chunk = keys[:, half].rearrange("p (c n) -> p c n", n=CHUNK)
                    step.did(V.tensor_tensor(by_chunk, by_chunk,
                                             column_number[:].unsqueeze(1).to_broadcast([ROWS, CHUNKS // 2, CHUNK]), ALU.mult))
                    if d == 0 and q is not None:
                        length = read_length(q)
                    step.wait()
                    for c in range(CHUNKS // 2):
                        i, rest = divmod(d * CHUNKS // 2 + c, CHUNKS // PICKS)
                        if n.k > 0 and rest == 0 and i < PICKS:
                            pick(n.plus(-1), i, step)
                        if (d, c) == (1, CHUNKS // 16) and n.k == 0 and not (isinstance(n.v, int) and n.number == 0):
                            place_rows(n.window - 1)
                        if (d, c) == (1, CHUNKS // 2 - 2) and isinstance(n.v, int) and n.number == WINDOW:
                            for j in range(2):
                                stage_record(Tile(0, j))
                        last = V.max(cand[:, d * CHUNKS // 2 + c, :], by_chunk[:, c, :])
                    last.then_inc(keys_used, 1)
                dve.wait_ge(keys_used, 2 * n.number + 4)
                base_b = chunk_base[:].unsqueeze(2).to_broadcast([ROWS, CHUNKS, 8])
                step(V.scalar_tensor_tensor(cand_base, cand, 0.0, base_b, ALU.is_gt, ALU.mult))
                if n.k > 0:
                    step.did(count(n.plus(-1)))
                step(V.tensor_tensor(cand, cand, cand_base, ALU.add))
                if n.k == WINDOW - 1:
                    for i in range(PICKS):
                        pick(n, i, step)
                    step.wait()
                    step(count(n))
                return length

            def split_x(w):
                step = Chain(dve, build_step)
                dve.wait_ge(x_window_loaded, ALL * (w + 1))
                dve.wait_ge(x_permuted, w + 1)
                step(V.tensor_tensor(x_rest[:], x_window[:], x_parts[0], ALU.subtract))
                V.tensor_tensor(x_last[:], x_rest[:], x_parts[1], ALU.subtract).then_inc(x_split, 1)

            def rank_window(w):
                step = Chain(dve, build_step)
                first = w * WINDOW
                V.tensor_copy(listed[:, bass.ds(first, WINDOW)], built[:, :, COUNT])
                V.tensor_copy(built[:, :, NODE:NODE1 + 1], node_number[:, bass.ds(first, WINDOW), :])
                step(V.scalar_tensor_tensor(sort_key[:], built[:, :, COUNT], float(PLACES), tie[:], ALU.mult, ALU.add))
                dve.wait_ge(sorted_done, w + 1)
                dve.wait_ge(x_permuted, w + 1)
                V.tensor_tensor(key_diag, ident[:].unsqueeze(1).to_broadcast([ROWS, WINDOW, ROWS]),
                                sort_key[:].unsqueeze(2).to_broadcast([ROWS, WINDOW, ROWS]), ALU.mult).then_inc(diag_made, 1)
                step(V.tensor_copy(built_int, built[:]))
                for d, bits in enumerate((NODES * 2 - DIGIT, DIGIT - 1)):
                    step(V.tensor_scalar(digit_int, built_int, bits, None, ALU.bitwise_and))
                    step(V.tensor_copy(digits[d][:], digit_int))
                dve.sem_inc(digits_made, 1)

            def place_rows(w):
                dve.wait_ge(standing_made, w + 1)
                for k in range(WINDOW):
                    last = V.tensor_scalar(onehot[:, k, :], place_number[:], standing[:, k:k + 1], None, ALU.is_equal)
                last.then_inc(onehots_made, 1)

            def stage_record(q):
                dve.wait_ge(records_made, q.window + 2)
                if not (isinstance(q.v, int) and q.number < 4):
                    dve.wait_ge(scattered[q.b], ALL * q.half)
                V.tensor_copy(stage[q.s][:], column(records, q.number)).then_inc(list_ready, 1)

            def post(s, b, stored_before, step):
                dve.wait_ge(mid_stored[b], stored_before)
                V.tensor_tensor(mid_t[b][:], x_t[b][:], nb_max[:], ALU.add).then_inc(mid_made, 1)
                dve.wait_ge(mid_made, s + 1)
                step(V.bn_stats(bn[:], mid_t[b][:]))
                V.bn_aggr(mean_var[:], bn[:]).then_inc(tile_var, 1)
                dve.wait_ge(tile_std, s + 1)
                step(V.reciprocal(rstd[:], std[:]))
                V.scalar_tensor_tensor(shift[:], mean_var[:, 0:1], -1.0, rstd[:], ALU.mult, ALU.mult).then_inc(shift_made, 1)

            expected = [dve.alloc_register(f"expected{b}") for b in range(2)]
            for b in range(2):
                dve.reg_mov(expected[b], 0)

            def landed(b, done, dmas):
                dve.reg_add(expected[b], expected[b], ALL * dmas)
                dve.wait_ge(done, dve.snap(expected[b]))
                dve.sem_inc(dve_holds, 1)

            def maximum(q, length):
                step = Chain(dve, post_step)

                def with_slots(slots):
                    landed(q.b, gathered[q.b], slots)
                    V.tensor_reduce(nb_max[:], gath[q.b][:, 0:slots, 0:FEAT].rearrange("p k f -> p f k"),
                                    AX.X, ALU.max).then_inc(max_made, 1)
                by_level(dve, length, LEVELS, with_slots)
                if not (isinstance(q.v, int) and q.number + 2 >= TILES):
                    stage_record(q.plus(2))
                dve.wait_ge(max_made, q.number + 1)
                dve.wait_ge(x_loaded[q.b], ALL * (q.half + 1))
                post(q.number, q.b, ALL * (q.half + 1), step)
                dve.wait_ge(mid_made, q.number + 1)
                dve.sem_inc(buffers_free, 1)

            def turn(n, q):
                if n is None and q.number + LEAD == TILES:
                    place_rows(TILES // WINDOW - 1)
                if n is not None:
                    length = build(n, q)
                    if n.k == WINDOW - 3:
                        split_x(n.window)
                    if n.k == WINDOW - 1:
                        rank_window(n.window)
                if q is None:
                    if n.number in (1, 2):
                        input_means(n.number - 1)
                    if n.number == 4:
                        input_shifts()
                    return
                maximum(q, length if n is not None else read_length(q))
            steps(dve, turn)

            step = Chain(dve, check_step)
            dve.wait_ge(squares_done, TILES + 2)
            step(V.tensor_scalar(bad[:], listed[:], 0.5, NODES / 16, ALU.mult, ALU.add))
            step(V.tensor_tensor(bad[:], bad[:], square_sum[:], ALU.not_equal))
            step(V.tensor_scalar(empty[:], listed[:], 0.0, None, ALU.is_equal))
            step(V.tensor_tensor(bad[:], bad[:], empty[:], ALU.max))
            step(V.tensor_reduce(bad_row[:], bad[:], AX.X, ALU.max))
            dve.sem_inc(bad_row_made, 1)
            dve.wait_ge(bad_summed, 1)
            V.tensor_copy(bad_count[:], p_bad).then_inc(verdict, 1)
            dve.wait_ge(verdict, 1)
            bad_rows = dve.value_load(bad_count[0:1, 0:1], min_val=0, max_val=ROWS)

            def finish(t, b, step, stored, value):
                step(V.reciprocal(total[:], total[:]))
                agg_h = agg.rearrange("p (h d) -> p h d", h=HEADS)
                step(V.tensor_tensor(agg_h, agg_h, total[:].unsqueeze(2).to_broadcast([ROWS, HEADS, HDIM]), ALU.mult))
                V.tensor_scalar(neg, agg, 0.0, None, ALU.min).then_inc(neg_made, 1)
                step(V.scalar_tensor_tensor(pos, agg, 0.0, mid_t[b][:], ALU.max, ALU.add))
                dve.wait_ge(neg_exped, t + 1)
                dve.wait_ge(stored, value)
                return V.scalar_tensor_tensor(out_t[b][:], neg_exp, -1.0, pos, ALU.add, ALU.add)

            def scores(t, b, slots, step):
                dst = gath[b][:, 0:slots, FEAT:GROW].rearrange("p k h -> p h k")
                e = score[:, :, 0:slots]
                step(V.tensor_tensor(e, dst, column(src_score, t).unsqueeze(2).to_broadcast([ROWS, HEADS, slots]), ALU.add))
                step(V.scalar_tensor_tensor(e, e, SLOPE, e, ALU.mult, ALU.max))

            def weigh(b, slots, step, into):
                g = gath[b][:, 0:slots, 0:FEAT]
                w = prob[:, :, 0:slots].rearrange("p h k -> p k h").unsqueeze(3).to_broadcast([ROWS, slots, HEADS, HDIM])
                g_h = g.rearrange("p k (h d) -> p k h d", h=HEADS)
                step(V.tensor_tensor(g_h, g_h, w, ALU.mult))
                return V.tensor_reduce(into, g.rearrange("p k f -> p f k"), AX.X, ALU.add)

            with dve.If(bad_rows == 0):
                dve.sem_inc(attn_buffers_free, 2)
                for b in range(2):
                    dve.reg_mov(expected[b], 0)
                step = Chain(dve, attn_step)
                step(V.memset(score, 0.0))

                def stage_list(q):
                    dve.wait_ge(scattered[q.b], ALL * (TILES // 2 + q.half))
                    V.tensor_copy(stage[q.s][:], column(records, q.number)).then_inc(stage_ready, 1)

                def attend(q):
                    t, b = q.number, q.b
                    dve.wait_ge(stage_ready, t + 1)
                    dve.sem_inc(dve_holds, 1)
                    length = longest(dve, q.s)

                    def with_slots(slots):
                        step = Chain(dve, attn_step)
                        landed(b, attn_gathered[b], slots)
                        e = score[:, :, 0:slots]
                        scores(t, b, slots, step)
                        step(V.tensor_reduce(peak[:], e, AX.X, ALU.max))
                        V.tensor_tensor(e, e, peak[:].unsqueeze(2).to_broadcast([ROWS, HEADS, slots]), ALU.subtract).then_inc(score_made, 1)
                        dve.wait_ge(prob_made, t + 1)
                        V.tensor_reduce(total[:], prob[:, :, 0:slots], AX.X, ALU.add)
                        weigh(b, slots, step, agg).then_inc(agg_made, 1)
                    by_level(dve, length, LEVELS, with_slots)
                    dve.wait_ge(agg_made, t + 1)
                    dve.sem_inc(attn_buffers_free, 1)
                    step = Chain(dve, attn_step)
                    dve.wait_ge(mid_loaded[b], ALL * (q.half + 1))
                    finish(t, b, step, scattered[b], ALL * (1 + TILES // 2 + q.half)).then_inc(out_ready, 1)
                    dve.wait_ge(out_ready, t + 1)
                    dve.sem_inc(out_made, 1)

                for b in range(2):
                    dve.wait_ge(scattered[b], ALL * (1 + TILES // 2))
                for j in range(2):
                    stage_list(Tile(0, j))

                def attn_turn(q):
                    if not (isinstance(q.v, int) and q.number + 2 >= TILES):
                        stage_list(q.plus(2))
                    attend(q)
                sorted_tiles(dve, attn_turn)
            with dve.Else():
                mask = adj_in[0][:].bitcast(f32)
                dve.sem_inc(dense_free, 2)
                dve.sem_inc(dense_mask_free, 1)
                dve.sem_inc(dense_out_stored, ALL)
                with dve.Fori(0, TILES) as t:
                    step = Chain(dve, dense_step)
                    dve.wait_ge(dense_adj_loaded, ALL * (t + 1))
                    step(V.tensor_scalar(mask, adj_in[0][:], 0.0, None, ALU.not_equal))
                    step(V.memset(nb_max[:], 0.0))
                    with dve.Fori(0, BLOCKS // 2) as c2:
                        for b in range(2):
                            step = Chain(dve, dense_step)
                            dve.wait_ge(dense_loaded[b], ALL * (t * (BLOCKS // 2) + c2 + 1))
                            g = gath[b][:, :, 0:FEAT]
                            m = mask[:, bass.ds((2 * c2 + b) * BLOCK, BLOCK)].unsqueeze(2).to_broadcast([ROWS, BLOCK, FEAT])
                            step(V.tensor_tensor(g, g, m, ALU.mult))
                            step(V.tensor_reduce(part, g.rearrange("p k f -> p f k"), AX.X, ALU.max))
                            step(V.tensor_tensor(nb_max[:], nb_max[:], part, ALU.max))
                            dve.sem_inc(dense_free, 1)
                    step = Chain(dve, post_step)
                    dve.wait_ge(dense_x_loaded, ALL * (t + 1))
                    post(t + TILES, 0, ALL * (1 + TILES // 2 + t), step)
                    dve.sem_inc(dense_mask_free, 1)

                agg_h = agg.rearrange("p (h d) -> p h d", h=HEADS)
                with dve.Fori(0, TILES) as t:
                    step = Chain(dve, dense_step)
                    dve.wait_ge(dense_adj_loaded, ALL * (t + 1 + TILES))
                    step(V.tensor_scalar(mask, adj_in[0][:], 0.0, None, ALU.is_gt))
                    step(V.memset(peak_new[:], -3.0e38))
                    step(V.memset(total[:], 0.0))
                    step(V.memset(agg, 0.0))
                    with dve.Fori(0, BLOCKS // 2) as c2:
                        for b in range(2):
                            step = Chain(dve, dense_step)
                            n = t * BLOCKS + 2 * c2 + b
                            dve.wait_ge(dense_loaded[b], ALL * (t * (BLOCKS // 2) + c2 + 1 + TILES * (BLOCKS // 2)))
                            m1 = mask[:, bass.ds((2 * c2 + b) * BLOCK, BLOCK)]
                            scores(t, b, BLOCK, step)
                            step(V.tensor_tensor(score, score, m1.unsqueeze(1).to_broadcast([ROWS, HEADS, BLOCK]), ALU.mult))
                            step(V.tensor_scalar(is_nb[:], m1, -1.0, MASKED, ALU.add, ALU.mult))
                            step(V.tensor_tensor(score, score, is_nb[:].unsqueeze(1).to_broadcast([ROWS, HEADS, BLOCK]), ALU.add))
                            step(V.tensor_copy(peak[:], peak_new[:]))
                            step(V.tensor_reduce(part_sum[:], score, AX.X, ALU.max))
                            step(V.tensor_tensor(peak_new[:], peak[:], part_sum[:], ALU.max))
                            step(V.tensor_tensor(peak[:], peak[:], peak_new[:], ALU.subtract))
                            V.tensor_tensor(score, score, peak_new[:].unsqueeze(2).to_broadcast([ROWS, HEADS, BLOCK]),
                                            ALU.subtract).then_inc(dense_score, 1)
                            dve.wait_ge(dense_exp, n + 1)
                            step(V.tensor_reduce(part_sum[:], prob, AX.X, ALU.add))
                            step(V.tensor_tensor(total[:], total[:], rescale[:], ALU.mult))
                            step(weigh(b, BLOCK, step, part))
                            step(V.tensor_tensor(total[:], total[:], part_sum[:], ALU.add))
                            step(V.tensor_tensor(agg_h, agg_h, rescale[:].unsqueeze(2).to_broadcast([ROWS, HEADS, HDIM]), ALU.mult))
                            step(V.tensor_tensor(agg, agg, part, ALU.add))
                            dve.sem_inc(dense_free, 1)
                    dve.wait_ge(mid_loaded[0], ALL * (t + 1))
                    finish(t, 0, step, dense_out_stored, ALL * (t + 1)).then_inc(out_made, 1)
                    dve.wait_ge(out_made, t + 1)
                    dve.sem_inc(dense_mask_free, 1)


def kernel(x, adj, L1_gnn_W, L1_gnn_a):
    import numpy as np
    import concourse.bacc as bacc
    from concourse.bass_utils import run_bass_kernel_spmd

    arrays = {"x": np.asarray(x), "adj": np.asarray(adj), "weight": np.asarray(L1_gnn_W), "attn": np.asarray(L1_gnn_a)}
    nc = bacc.Bacc("TRN2", target_bir_lowering=False, num_devices=1)
    args = [nc.dram_tensor(n, a.shape, mybir.dt.from_np(a.dtype), kind="ExternalInput").ap() for n, a in arrays.items()]
    out = nc.dram_tensor("out", (NODES, FEAT), mybir.dt.float32, kind="ExternalOutput").ap()
    gnn_program(nc, *args, out)
    return run_bass_kernel_spmd(nc, [arrays], core_ids=[0]).results[0]["out"]
```
